# Optimizing a Trainium2 kernel written in Bass

```python
import numpy as np
import jax
import jax.numpy as jnp

def _softmax(x, axis=-1):
    return jax.nn.softmax(x, axis=axis)

def _gelu(x):
    return jax.nn.gelu(x, approximate=True)

def _silu(x):
    return jax.nn.silu(x)

def _sigmoid(x):
    return jax.nn.sigmoid(x)

def _layernorm(x, axis=-1, eps=1e-05):
    m = jnp.mean(x, axis=axis, keepdims=True)
    v = jnp.var(x, axis=axis, keepdims=True)
    return (x - m) / jnp.sqrt(v + eps)

def _scatter_add(tgt, idx, src, axis=0):
    return tgt.at[idx].add(src)

def _segment_sum(src, seg, n):
    return jax.ops.segment_sum(src, seg, n)
kernel_name = 'mk_sandwich_d1_jaxref_r8_2de588'

def setup_inputs(seed: int=0):
    np.random.seed(seed)
    _w = jnp.asarray

    def _L0_attn_setup():
        import jax, jax.numpy as jnp
        import numpy as np
        import math
        D_MODEL = 128
        D_STATE = 16
        EXPAND = 2
        D_CONV = 4
        D_INNER = EXPAND * D_MODEL
        DT_RANK = math.ceil(D_MODEL / 16)
        B_SZ, L_SEQ = (2, 256)

        def _layernorm(x, g, b, eps=1e-05):
            mu = jnp.mean(x, -1, keepdims=True)
            var = jnp.var(x, -1, keepdims=True)
            return (x - mu) * jax.lax.rsqrt(var + eps) * g + b

        def _causal_depthwise_conv(x, w, b):
            K = w.shape[1]
            xp = jnp.pad(x, ((0, 0), (K - 1, 0), (0, 0)))
            L = x.shape[1]
            y = sum((xp[:, k:k + L, :] * w[:, k] for k in range(K)))
            return y + b

        def _selective_scan(u, dt, A, Bm, Cm, D):
            dA = jnp.exp(dt[..., None] * A)
            dBu = (dt * u)[..., None] * Bm[:, :, None, :]

            def combine(e1, e2):
                a1, b1 = e1
                a2, b2 = e2
                return (a2 * a1, a2 * b1 + b2)
            _, h = jax.lax.associative_scan(combine, (dA, dBu), axis=1)
            y = jnp.einsum('blds,bls->bld', h, Cm)
            return y + u * D

        def _mamba(x, in_proj_w, conv_w, conv_b, x_proj_w, dt_proj_w, dt_proj_b, A_log, D, out_proj_w):
            xz = jnp.einsum('bld,ed->ble', x, in_proj_w)
            xin, z = jnp.split(xz, 2, axis=-1)
            xc = jax.nn.silu(_causal_depthwise_conv(xin, conv_w, conv_b))
            dbl = jnp.einsum('bld,ed->ble', xc, x_proj_w)
            dt, Bm, Cm = jnp.split(dbl, [DT_RANK, DT_RANK + D_STATE], axis=-1)
            dt = jax.nn.softplus(jnp.einsum('blr,dr->bld', dt, dt_proj_w) + dt_proj_b)
            A = -jnp.exp(A_log)
            y = _selective_scan(xc, dt, A, Bm, Cm, D)
            y = y * jax.nn.silu(z)
            return jnp.einsum('bld,ed->ble', y, out_proj_w)
        key = jax.random.key(seed)
        ks = jax.random.split(key, 10)
        s = 0.02
        inp = {'x': jax.random.normal(ks[0], (B_SZ, L_SEQ, D_MODEL), jnp.float32), 'ln_gamma': jnp.ones((D_MODEL,), jnp.float32), 'ln_beta': jnp.zeros((D_MODEL,), jnp.float32), 'in_proj_w': jax.random.normal(ks[1], (2 * D_INNER, D_MODEL), jnp.float32) * s, 'conv_w': jax.random.normal(ks[2], (D_INNER, D_CONV), jnp.float32) * s, 'conv_b': jnp.zeros((D_INNER,), jnp.float32), 'x_proj_w': jax.random.normal(ks[3], (DT_RANK + 2 * D_STATE, D_INNER), jnp.float32) * s, 'dt_proj_w': jax.random.normal(ks[4], (D_INNER, DT_RANK), jnp.float32) * DT_RANK ** (-0.5), 'dt_proj_b': jnp.full((D_INNER,), float(np.log(np.expm1(0.01))), jnp.float32), 'A_log': jnp.log(jnp.broadcast_to(jnp.arange(1, D_STATE + 1, dtype=jnp.float32), (D_INNER, D_STATE))), 'D': jnp.ones((D_INNER,), jnp.float32), 'out_proj_w': jax.random.normal(ks[5], (D_MODEL, D_INNER), jnp.float32) * s}
        return inp
    _L0_attn_in = _L0_attn_setup()

    def _L0_ffn_setup():
        import jax, jax.numpy as jnp
        import numpy as np
        DIM = 128

        def _reference_tuple_inner(x, W_r, W_k, W_v, mu_r, mu_k):
            B, T, C = x.shape
            x_prev = jnp.concatenate([jnp.zeros((B, 1, C), x.dtype), x[:, :-1, :]], axis=1)
            xr = mu_r * x + (1.0 - mu_r) * x_prev
            xk = mu_k * x + (1.0 - mu_k) * x_prev
            r = jax.nn.sigmoid(jnp.einsum('btc,dc->btd', xr, W_r))
            k = jnp.einsum('btc,dc->btd', xk, W_k)
            k_act = jnp.square(jax.nn.relu(k))
            out = r * jnp.einsum('btc,dc->btd', k_act, W_v)
            new_state = x[:, -1, :]
            return (out, new_state)
        key = jax.random.key(seed)
        ks = jax.random.split(key, 6)
        B, T, C = (8, 256, DIM)
        x = jax.random.normal(ks[0], (B, T, C), dtype=jnp.float32)
        s = 1.0 / np.sqrt(C)
        W_r = jax.random.uniform(ks[1], (C, C), jnp.float32, -s, s)
        W_k = jax.random.uniform(ks[2], (C, C), jnp.float32, -s, s)
        W_v = jax.random.uniform(ks[3], (C, C), jnp.float32, -s, s)
        mu_r = jax.random.uniform(ks[4], (C,), jnp.float32)
        mu_k = jax.random.uniform(ks[5], (C,), jnp.float32)
        return {'x': x, 'W_r': W_r, 'W_k': W_k, 'W_v': W_v, 'mu_r': mu_r, 'mu_k': mu_k}
    _L0_ffn_in = _L0_ffn_setup()
    _d = {'L0_attn_x': _L0_attn_in['x'], 'L0_attn_ln_gamma': _L0_attn_in['ln_gamma'], 'L0_attn_ln_beta': _L0_attn_in['ln_beta'], 'L0_attn_in_proj_w': _L0_attn_in['in_proj_w'], 'L0_attn_conv_w': _L0_attn_in['conv_w'], 'L0_attn_conv_b': _L0_attn_in['conv_b'], 'L0_attn_x_proj_w': _L0_attn_in['x_proj_w'], 'L0_attn_dt_proj_w': _L0_attn_in['dt_proj_w'], 'L0_attn_dt_proj_b': _L0_attn_in['dt_proj_b'], 'L0_attn_A_log': _L0_attn_in['A_log'], 'L0_attn_D': _L0_attn_in['D'], 'L0_attn_out_proj_w': _L0_attn_in['out_proj_w'], 'L0_ffn_W_r': _L0_ffn_in['W_r'], 'L0_ffn_W_k': _L0_ffn_in['W_k'], 'L0_ffn_W_v': _L0_ffn_in['W_v'], 'L0_ffn_mu_r': _L0_ffn_in['mu_r'], 'L0_ffn_mu_k': _L0_ffn_in['mu_k']}
    _x0 = _d['L0_attn_x']
    _d['L0_attn_x'] = jax.random.normal(jax.random.fold_in(jax.random.key(seed), 1), (16, 512, 128), dtype=_x0.dtype)
    del _x0
    return _d

def reference(L0_attn_x, L0_attn_ln_gamma, L0_attn_ln_beta, L0_attn_in_proj_w, L0_attn_conv_w, L0_attn_conv_b, L0_attn_x_proj_w, L0_attn_dt_proj_w, L0_attn_dt_proj_b, L0_attn_A_log, L0_attn_D, L0_attn_out_proj_w, L0_ffn_W_r, L0_ffn_W_k, L0_ffn_W_v, L0_ffn_mu_r, L0_ffn_mu_k):

    def _L0_attn_ref(x, ln_gamma, ln_beta, in_proj_w, conv_w, conv_b, x_proj_w, dt_proj_w, dt_proj_b, A_log, D, out_proj_w):
        import jax, jax.numpy as jnp
        import numpy as np
        import math
        D_MODEL = 128
        D_STATE = 16
        EXPAND = 2
        D_CONV = 4
        D_INNER = EXPAND * D_MODEL
        DT_RANK = math.ceil(D_MODEL / 16)
        B_SZ, L_SEQ = (2, 256)

        def _layernorm(x, g, b, eps=1e-05):
            mu = jnp.mean(x, -1, keepdims=True)
            var = jnp.var(x, -1, keepdims=True)
            return (x - mu) * jax.lax.rsqrt(var + eps) * g + b

        def _causal_depthwise_conv(x, w, b):
            K = w.shape[1]
            xp = jnp.pad(x, ((0, 0), (K - 1, 0), (0, 0)))
            L = x.shape[1]
            y = sum((xp[:, k:k + L, :] * w[:, k] for k in range(K)))
            return y + b

        def _selective_scan(u, dt, A, Bm, Cm, D):
            dA = jnp.exp(dt[..., None] * A)
            dBu = (dt * u)[..., None] * Bm[:, :, None, :]

            def combine(e1, e2):
                a1, b1 = e1
                a2, b2 = e2
                return (a2 * a1, a2 * b1 + b2)
            _, h = jax.lax.associative_scan(combine, (dA, dBu), axis=1)
            y = jnp.einsum('blds,bls->bld', h, Cm)
            return y + u * D

        def _mamba(x, in_proj_w, conv_w, conv_b, x_proj_w, dt_proj_w, dt_proj_b, A_log, D, out_proj_w):
            xz = jnp.einsum('bld,ed->ble', x, in_proj_w)
            xin, z = jnp.split(xz, 2, axis=-1)
            xc = jax.nn.silu(_causal_depthwise_conv(xin, conv_w, conv_b))
            dbl = jnp.einsum('bld,ed->ble', xc, x_proj_w)
            dt, Bm, Cm = jnp.split(dbl, [DT_RANK, DT_RANK + D_STATE], axis=-1)
            dt = jax.nn.softplus(jnp.einsum('blr,dr->bld', dt, dt_proj_w) + dt_proj_b)
            A = -jnp.exp(A_log)
            y = _selective_scan(xc, dt, A, Bm, Cm, D)
            y = y * jax.nn.silu(z)
            return jnp.einsum('bld,ed->ble', y, out_proj_w)
        h = _layernorm(x, ln_gamma, ln_beta)
        return x + _mamba(h, in_proj_w, conv_w, conv_b, x_proj_w, dt_proj_w, dt_proj_b, A_log, D, out_proj_w)

    def _L0_ffn_ref(x, W_r, W_k, W_v, mu_r, mu_k):
        import jax, jax.numpy as jnp
        import numpy as np
        DIM = 128

        def _reference_tuple_inner(x, W_r, W_k, W_v, mu_r, mu_k):
            B, T, C = x.shape
            x_prev = jnp.concatenate([jnp.zeros((B, 1, C), x.dtype), x[:, :-1, :]], axis=1)
            xr = mu_r * x + (1.0 - mu_r) * x_prev
            xk = mu_k * x + (1.0 - mu_k) * x_prev
            r = jax.nn.sigmoid(jnp.einsum('btc,dc->btd', xr, W_r))
            k = jnp.einsum('btc,dc->btd', xk, W_k)
            k_act = jnp.square(jax.nn.relu(k))
            out = r * jnp.einsum('btc,dc->btd', k_act, W_v)
            new_state = x[:, -1, :]
            return (out, new_state)
        return _reference_tuple_inner(x, W_r, W_k, W_v, mu_r, mu_k)[0]
    x = L0_attn_x
    x = x + _layernorm(_L0_attn_ref(_layernorm(x, axis=-1), L0_attn_ln_gamma, L0_attn_ln_beta, L0_attn_in_proj_w, L0_attn_conv_w, L0_attn_conv_b, L0_attn_x_proj_w, L0_attn_dt_proj_w, L0_attn_dt_proj_b, L0_attn_A_log, L0_attn_D, L0_attn_out_proj_w), axis=-1)
    x = x + _layernorm(_L0_ffn_ref(_layernorm(x, axis=-1), L0_ffn_W_r, L0_ffn_W_k, L0_ffn_W_v, L0_ffn_mu_r, L0_ffn_mu_k), axis=-1)
    return x

_drawn_inputs = setup_inputs


def setup_inputs(seed=0):
    import zlib

    import numpy as np

    out = dict(_drawn_inputs(seed))
    spreads = {'L0_attn_ln_gamma': (1.0, 0.6),
     'L0_attn_ln_beta': (0.0, 0.8),
     'L0_attn_conv_b': (0.0, 0.8),
     'L0_attn_dt_proj_b': (-4.600165843963623, 0.6),
     'L0_attn_D': (1.0, 0.6)}
    factors = {'L0_attn_in_proj_w': 8.0,
     'L0_attn_conv_w': 8.0,
     'L0_attn_x_proj_w': 8.0,
     'L0_attn_dt_proj_w': 8.0,
     'L0_attn_A_log': 8.0,
     'L0_attn_out_proj_w': 8.0}
    for name, (base, spread) in spreads.items():
        noise = np.random.default_rng([zlib.crc32(name.encode()), seed]).standard_normal(out[name].shape)
        drawn = base * np.exp(spread * noise) if base else spread * noise
        out[name] = jnp.asarray(drawn.astype(out[name].dtype))
    for name, factor in factors.items():
        out[name] = (out[name] * factor).astype(out[name].dtype)
    return out
```

```python
from contextlib import ExitStack

import concourse.bass as bass
from concourse import mybir

FP32 = mybir.dt.float32
BF16 = mybir.dt.bfloat16
ALU = mybir.AluOpType
ACT = mybir.ActivationFunctionType

EPS = 1e-5
EXP_LN_SET = "natural_log_exp_and_others"
P = 128
L = 512
S = 16
HALVES = 2
TAPS = 4
RANK = 8
TILES = L // P
PT = 2 * TILES
STEPS = 2 * S
LAG = 2

GROUPS = ["outproj1", "front_tr0", "front_tr1", "conv00", "conv01", "conv10", "conv11",
          "z00", "z01", "z10", "z11", "back_tr0", "back_tr1", "key0", "key1", "gate0", "gate1",
          "xproj0", "xproj1", "outproj0", "dt00", "dt01", "dt10", "dt11", "value0", "value1"]
PER_BANK = len(GROUPS) // 2


def bank_of(group):
    return GROUPS.index(group) % 2


def count_of(group, w):
    return w * PER_BANK + (GROUPS.index(group) // 2 + 1)


def wait(engine, semaphore, value):
    if not isinstance(value, int) or value > 0:
        engine.wait_ge(semaphore, value)


def mamba_sandwich(nc, x, ln_gamma, ln_beta, in_proj_w, conv_w, conv_b, x_proj_w, dt_proj_w,
                   dt_proj_b, A_log, D, out_proj_w, W_r, W_k, W_v, mu_r, mu_k, out):
    pairs = x.shape[0] // 2
    x_pairs = x.rearrange("(w b) (j p) d -> w p (b j) d", b=2, p=P)
    out_pairs = out.rearrange("(w b) (j p) d -> w p (b j) d", b=2, p=P)

    ctx = ExitStack()
    with ctx:
        def sb(name, shape, dt=FP32):
            return ctx.enter_context(nc.sbuf_tensor(name, shape, dt))

        def sem(name):
            return ctx.enter_context(nc.semaphore(name))

        in_w = sb("in_w", [P, 4, P])
        conv_taps = sb("conv_taps", [P, HALVES, TAPS])
        conv_bias = sb("conv_bias", [P, HALVES])
        xp_rows = sb("xp_rows", [P, HALVES * P])
        dt_w_rows = sb("dt_w_rows", [P, HALVES, RANK])
        dt_bias = sb("dt_bias", [P, HALVES])
        a_log = sb("a_log", [P, HALVES, S])
        d_skip = sb("d_skip", [P, HALVES])
        out_w = sb("out_w", [P, HALVES * P])
        mix_w = sb("mix_w", [P, 3, P])
        mix_mu = sb("mix_mu", [P, 2])
        gamma_beta = sb("gamma_beta", [P, 2])

        ident = sb("ident", [P, P])
        ident_bf = sb("ident_bf", [P, P], BF16)
        pick = sb("pick", [P, 2 * S], BF16)
        spread = sb("spread", [P, 2 * S, P], BF16)
        eps_col = sb("eps_col", [P, 1])
        one_col = sb("one_col", [P, 1])
        tap_wT = sb("tap_wT", [P, HALVES, TAPS, P])
        z_wT = sb("z_wT", [P, HALVES, P])
        xp_wT = sb("xp_wT", [P, HALVES, P])
        dt_wT = sb("dt_wT", [RANK, HALVES, P])
        neg_a = sb("neg_a", [P, HALVES, S])
        out_wT = sb("out_wT", [P, HALVES, P])
        mix_wT = sb("mix_wT", [P, 3, P])
        one_minus_mu = sb("one_minus_mu", [P, 2])
        mix_now = sb("mix_now", [P, 2, P])
        mix_before = sb("mix_before", [P, 2, P])

        xf = sb("xf", [P, PT, P])
        hn = sb("hn", [P, PT, P])
        tap_w = hn[:].rearrange("p (h k) d -> p h k d", h=HALVES)
        hT = sb("hT", [P, 2, L])
        xc = [sb(f"xc{i}", [P, HALVES, 2, L]) for i in range(2)]
        zs = [sb(f"zs{i}", [P, HALVES, 2, L]) for i in range(2)]
        dt = [sb(f"dt{i}", [P, HALVES, 2, L]) for i in range(2)]
        dtu = [sb(f"dtu{i}", [P, HALVES, 2, L]) for i in range(2)]
        parts = [sb(f"parts{i}", [P, 2, L], BF16) for i in range(2)]
        rest = sb("rest", [P, 2, L])
        dt_low = sb("dt_low", [RANK, 2, L])
        soft = sb("soft", [P, 2, HALVES, L])
        soft_ln = sb("soft_ln", [P, HALVES, L])
        soft_lin = sb("soft_lin", [P, HALVES, L])

        dbu = sb("dbu", [P, 2, HALVES, L])
        h = sb("h", [P, 4, HALVES, L])
        c_sb = sb("c_sb", [P, 4, L])
        prod = sb("prod", [P, 2, HALVES, L])

        xb = sb("xb", [P, PT, P])
        yg = sb("yg", [P, HALVES, L])
        v = sb("v", [P, PT, P])
        x1 = sb("x1", [P, PT, P])
        f = v
        fT = sb("fT", [P, 2, L + 1])
        key = sb("key", [P, 2, L])
        gate = sb("gate", [P, PT, P])
        o = sb("o", [P, PT, P])

        def stat_tiles(name):
            return {k: sb(f"{name}_{k}", [P, PT] + ([6] if k == "bn" else []))
                    for k in ("bn", "sum2", "dif", "m2", "sq", "var", "ln", "rstd", "shift")}

        st_front, st_attn, st_mid, st_out = (stat_tiles(n) for n in ("front", "attn", "mid", "out"))
        r1 = [sb(f"r1_{i}", [P, PT]) for i in range(2)]
        r1_sq = sb("r1_sq", [P, PT])
        var_u = sb("var_u", [P, PT])
        ln_u = sb("ln_u", [P, PT])
        r2 = sb("r2", [P, PT])
        r1_back = sb("r1_back", [P, PT])

        bank = [ctx.enter_context(nc.psum_tensor(f"bank{i}", [P, L], FP32)) for i in range(8)]
        misc, da, y_acc, b_ps, c_ps = bank[0:2], bank[2:4], bank[4:6], bank[6], bank[7]

        weights_in, weights_cleared = sem("weights_in"), sem("weights_cleared")
        ident_made, consts_made, scaled_w = sem("ident_made"), sem("consts_made"), sem("scaled_w")
        w_transposed, w_drained, a_made = sem("w_transposed"), sem("w_drained"), sem("a_made")
        spread_made, mix_made = sem("spread_made"), sem("mix_made")
        filled = [sem("misc_filled0"), sem("misc_filled1")]
        drained = [sem("misc_drained0"), sem("misc_drained1")]
        xf_in, xb_in, out_stored = sem("xf_in"), sem("xb_in"), sem("out_stored")
        front_stat, front_rstd, hn_made = sem("front_stat"), sem("front_rstd"), sem("hn_made")
        silu_made, key_squared, soft_exp, ln_made = sem("silu_made"), sem("key_squared"), sem("soft_exp"), sem("ln_made")
        hi_made, parts_made, soft_made, dtu_made = sem("hi_made"), sem("parts_made"), sem("soft_made"), sem("dtu_made")
        b_spread, c_spread, c_copied = sem("b_spread"), sem("c_spread"), sem("c_copied")
        da_made, dbu_made, scanned = sem("da_made"), sem("dbu_made"), sem("scanned")
        prod_made, y_added = sem("prod_made"), sem("y_added")
        y_taken, y_gated, r1_kept, v_made = sem("y_taken"), sem("y_gated"), sem("r1_kept"), sem("v_made")
        attn_stat, attn_rstd, x1_scaled, x1_made = sem("attn_stat"), sem("attn_rstd"), sem("x1_scaled"), sem("x1_made")
        mid_stat, mid_rstd, f_made = sem("mid_stat"), sem("mid_rstd"), sem("f_made")
        out_stat, out_rstd, o_scaled, out_made = sem("out_stat"), sem("out_rstd"), sem("o_scaled"), sem("out_made")
        front_shift, attn_shift, mid_shift, out_shift = (sem(f"{n}_shift") for n in ("front", "attn", "mid", "out"))

        def bodies(engine, body):
            body(0, 0, front=True, scan=False, back=False)
            body(1, 1, front=True, scan=True, back=False)
            with engine.Fori(2, pairs, 2) as w:
                body(w, 0, front=True, scan=True, back=True)
                body(w + 1, 1, front=True, scan=True, back=True)
            body(pairs, 0, front=False, scan=True, back=True)
            body(pairs + 1, 1, front=False, scan=False, back=True)

        block = ctx.enter_context(nc.Block())

        @block.sync
        def _(sp):
            
            def load_column(dst, vector):
                sp.dma_start(dst, vector.rearrange("(h p) -> p h", p=P),
                             allow_slow_non_contiguous=True).then_inc(weights_in, 16)

            sp.dma_start(xf[:], x_pairs[0]).then_inc(xf_in, 16)
            sp.sem_inc(out_stored, 16)
            sp.dma_start(in_w[:], in_proj_w.rearrange("(c p) d -> p c d", p=P)).then_inc(weights_in, 16)
            sp.dma_start(conv_taps[:], conv_w.rearrange("(h p) k -> p h k", p=P)).then_inc(weights_in, 16)
            load_column(conv_bias[:], conv_b)
            sp.dma_start(dt_w_rows[:], dt_proj_w.rearrange("(h p) r -> p h r", p=P)).then_inc(weights_in, 16)
            load_column(dt_bias[:], dt_proj_b)
            sp.dma_start(a_log[:], A_log.rearrange("(h p) s -> p h s", p=P)).then_inc(weights_in, 16)
            load_column(d_skip[:], D)
            sp.dma_start(out_w[:], out_proj_w).then_inc(weights_in, 16)
            for i, wt in enumerate((W_r, W_k, W_v)):
                sp.dma_start(mix_w[:, i, :], wt).then_inc(weights_in, 16)
            for i, mu in enumerate((mu_r, mu_k)):
                load_column(mix_mu[:, i:i + 1], mu)
            for i, g in enumerate((ln_gamma, ln_beta)):
                load_column(gamma_beta[:, i:i + 1], g)
            sp.wait_ge(weights_cleared, 1)
            sp.dma_start(xp_rows[0:RANK, :], x_proj_w[0:RANK, :]).then_inc(weights_in, 16)
            for i in range(1, 4):
                sp.dma_start(xp_rows[32 * i:32 * i + 2 * S, :],
                             x_proj_w[RANK:RANK + 2 * S, :]).then_inc(weights_in, 16)

            def body(w, par, front, scan, back):
                if front and not (isinstance(w, int) and w >= pairs - 1):
                    sp.wait_ge(hn_made, w + 1)
                    sp.dma_start(xf[:], x_pairs[w + 1]).then_inc(xf_in, 16)
                if scan:
                    wait(sp, x1_made, w - 1)
                    sp.dma_start(xb[:], x_pairs[w - 1]).then_inc(xb_in, 16)
                if back:
                    sp.wait_ge(out_made, w)
                    sp.dma_start(out_pairs[w - 2], o[:]).then_inc(out_stored, 16)

            body(0, 0, True, False, False)
            body(1, 1, True, True, False)
            with sp.Fori(2, pairs - 2, 2) as w:
                body(w, 0, True, True, True)
                body(w + 1, 1, True, True, True)
            body(pairs - 2, 0, True, True, True)
            body(pairs - 1, 1, True, True, True)
            body(pairs, 0, False, True, True)
            body(pairs + 1, 1, False, False, True)
            sp.wait_ge(out_stored, 16 * (pairs + 1))

        @block.gpsimd
        def _(pool):
            nc.gpsimd.memset(ident[:], 0.0).then_inc(ident_made, 1)
            pool.wait_ge(ident_made, 1)
            nc.gpsimd.affine_select(out=ident[:], in_=ident[:], compare_op=ALU.not_equal, fill=1.0,
                                    base=0, pattern=[[-1, P]], channel_multiplier=1).then_inc(ident_made, 1)
            pool.sem_inc(out_made, 1)

            def body(w, par, front, scan, back):
                for n in range(STEPS):
                    if scan:
                        t = (w - 1) * STEPS + n
                        pool.wait_ge(scanned, 2 * t + 2)
                        pool.wait_ge(c_copied, t + 1)
                        wait(pool, y_added, t - 1)
                        nc.gpsimd.tensor_tensor(
                            prod[:, n % 2], h[:, n % 4],
                            c_sb[:, n % 4].unsqueeze(1).to_broadcast([P, HALVES, L]),
                            ALU.mult).then_inc(prod_made, 1)
                    if n == 3 and back:
                        pool.wait_ge(y_taken, 2 * (w - 2) + 2)
                        nc.gpsimd.tensor_tensor(yg[:], yg[:], zs[par][:, :, 1, :], ALU.mult).then_inc(y_gated, 1)
                    if n == 9 and back:
                        pool.wait_ge(x1_scaled, w - 1)
                        pool.wait_ge(xb_in, 16 * (w - 1))
                        nc.gpsimd.tensor_tensor(x1[:], x1[:], xb[:], ALU.add).then_inc(x1_made, 1)
                    if n == 19 and scan:
                        pool.wait_ge(y_taken, 2 * (w - 1) + 1)
                        nc.gpsimd.tensor_tensor(yg[:], yg[:], zs[1 - par][:, :, 0, :], ALU.mult).then_inc(y_gated, 1)
                    if n in (24, 26) and front:
                        bi = (n - 24) // 2
                        pool.wait_ge(soft_made, 6 * w + 3 * bi + 3)
                        nc.gpsimd.tensor_tensor(dt[par][:, :, bi, :], dt[par][:, :, bi, :], soft[:, bi],
                                                ALU.add).then_inc(dtu_made, 1)
                        pool.wait_ge(dtu_made, 4 * w + 2 * bi + 1)
                        pool.wait_ge(silu_made, 2 * w + 1)
                        nc.gpsimd.tensor_tensor(dtu[par][:, :, bi, :], dt[par][:, :, bi, :],
                                                xc[par][:, :, bi, :], ALU.mult).then_inc(dtu_made, 1)
                    if n == 29 and back:
                        pool.wait_ge(o_scaled, w - 1)
                        nc.gpsimd.tensor_tensor(o[:], o[:], x1[:], ALU.add).then_inc(out_made, 1)

            bodies(pool, body)

        @block.scalar
        def _(act):
            nc.scalar.preload_act_table_set(EXP_LN_SET)
            act.wait_ge(consts_made, 1)
            act.wait_ge(weights_in, 19 * 16)
            nc.scalar.activation(neg_a[:], a_log[:], ACT.Exp).then_inc(a_made, 1)

            def rstd(out_, ln_, var_, semaphore, base):
                nc.scalar.activation(ln_[:], var_[:], ACT.Ln, bias=eps_col[:], scale=1.0 / P).then_inc(semaphore, 1)
                act.wait_ge(semaphore, base + 1)
                nc.scalar.activation(out_[:], ln_[:], ACT.Exp, scale=-0.5).then_inc(semaphore, 1)

            def evacuate(group, w, out_, func, **kw):
                b = bank_of(group)
                act.wait_ge(filled[b], count_of(group, w))
                nc.scalar.activation(out_, misc[b][:], func, **kw).then_inc(drained[b], 1)

            def body(w, par, front, scan, back):
                for n in range(STEPS):
                    if scan:
                        t = (w - 1) * STEPS + n
                        bi, s = n // S, n % S
                        if n % S == 0:
                            act.wait_ge(dtu_made, 4 * (w - 1) + 2 * bi + 1)
                        for half in range(HALVES):
                            wait(act, scanned, 2 * t - 1 + half)
                            nc.scalar.activation(da[half][:], dt[1 - par][:, half, bi, :], ACT.Exp,
                                                 scale=neg_a[:, half, s:s + 1]).then_inc(da_made, 1)
                            if half == 0:
                                act.wait_ge(c_spread, t + 1)
                                wait(act, prod_made, t - 3)
                                nc.scalar.activation(c_sb[:, n % 4], c_ps[:], ACT.Copy).then_inc(c_copied, 1)
                    if n == 1 and front:
                        act.wait_ge(front_stat, 6 * w + 4)
                        rstd(r1[par], st_front["ln"], st_front["var"], front_rstd, 4 * w)
                    if n == 3 and front:
                        act.wait_ge(front_stat, 6 * w + 6)
                        rstd(r2, ln_u, var_u, front_rstd, 4 * w + 2)
                    if n == 6 and front:
                        for bi in range(2):
                            evacuate(f"front_tr{bi}", w, hT[:, bi, :], ACT.Identity,
                                     bias=gamma_beta[:, 1:2], scale=gamma_beta[:, 0:1])
                    if n == 7 and back:
                        act.wait_ge(attn_stat, 4 * (w - 1))
                        rstd(st_attn["rstd"], st_attn["ln"], st_attn["var"], attn_rstd, 2 * (w - 2))
                    if 8 <= n < 12 and front:
                        bi, half = (n - 8) // 2, (n - 8) % 2
                        if n == 8:
                            wait(act, y_taken, 2 * (w - 1))
                        evacuate(f"conv{bi}{half}", w, xc[par][:, half, bi, :], ACT.Identity,
                                 bias=conv_bias[:, half:half + 1])
                    if n == 11 and back:
                        act.wait_ge(mid_stat, 4 * (w - 1))
                        rstd(st_mid["rstd"], st_mid["ln"], st_mid["var"], mid_rstd, 2 * (w - 2))
                    if n in (12, 13) and front:
                        bi = n - 12
                        if bi == 0:
                            wait(act, y_gated, 2 * (w - 1))
                        for half in range(HALVES):
                            evacuate(f"z{bi}{half}", w, zs[par][:, half, bi, :], ACT.Identity)
                    if n == 14 and back:
                        for bi in range(2):
                            evacuate(f"back_tr{bi}", w, fT[:, bi, 1:L + 1], ACT.Identity)
                    if n == 16 and back:
                        for bi in range(2):
                            evacuate(f"key{bi}", w, key[:, bi, :], ACT.Relu)
                    if n == 18:
                        if back:
                            act.wait_ge(drained[bank_of("key1")], count_of("key1", w))
                            act.wait_ge(drained[bank_of("key0")], count_of("key0", w))
                            nc.scalar.activation(key[:], key[:], ACT.Square).then_inc(key_squared, 1)
                        if front:
                            for b in range(2):
                                act.wait_ge(drained[b], count_of(("z10", "z11")[b ^ bank_of("z10")], w))
                            nc.scalar.activation(xc[par][:], xc[par][:], ACT.Silu).then_inc(silu_made, 1)
                            nc.scalar.activation(zs[par][:], zs[par][:], ACT.Silu).then_inc(silu_made, 1)
                        if back:
                            for bi in range(2):
                                evacuate(f"gate{bi}", w, gate[:, bi * TILES:(bi + 1) * TILES, :], ACT.Sigmoid)
                        nc.scalar.preload_act_table_set(EXP_LN_SET)
                    if n == 20 and front:
                        for bi in range(2):
                            g = f"xproj{bi}"
                            act.wait_ge(filled[bank_of(g)], count_of(g, w))
                            nc.scalar.activation(dt_low[:, bi, :], misc[bank_of(g)][0:RANK, :], ACT.Copy)
                            nc.scalar.activation(parts[par][:, bi, :], misc[bank_of(g)][:],
                                                 ACT.Copy).then_inc(hi_made, 1)
                    if n in (22, 24) and front:
                        bi = (n - 22) // 2
                        for half in range(HALVES):
                            g = f"dt{bi}{half}"
                            b = bank_of(g)
                            act.wait_ge(filled[b], count_of(g, w))
                            nc.scalar.activation(soft[:, bi, half], misc[b][:], ACT.Abs,
                                                 bias=dt_bias[:, half:half + 1])
                            nc.scalar.activation(dt[par][:, half, bi, :], misc[b][:], ACT.Relu,
                                                 bias=dt_bias[:, half:half + 1]).then_inc(drained[b], 1)
                        act.wait_ge(drained[b], count_of(g, w))
                        nc.scalar.activation(soft[:, bi], soft[:, bi], ACT.Exp, scale=-1.0).then_inc(soft_exp, 1)
                        act.wait_ge(soft_exp, 2 * w + bi + 1)
                        wait(act, soft_made, 6 * w + 3 * bi)
                        nc.scalar.activation(soft_ln[:], soft[:, bi], ACT.Ln, bias=one_col[:]).then_inc(ln_made, 1)
                    if n == 27 and back:
                        act.wait_ge(out_stat, 4 * (w - 1))
                        rstd(st_out["rstd"], st_out["ln"], st_out["var"], out_rstd, 2 * (w - 2))

            bodies(act, body)

        @block.vector
        def _(dve):
            nc.vector.memset(xp_rows[:], 0.0).then_inc(weights_cleared, 1)
            nc.vector.memset(eps_col[:], EPS)
            nc.vector.memset(one_col[:], 1.0)
            nc.vector.memset(fT[:, :, 0:1], 0.0).then_inc(consts_made, 1)
            dve.wait_ge(ident_made, 2)
            nc.vector.tensor_copy(ident_bf[:], ident[:]).then_inc(spread_made, 1)
            dve.wait_ge(spread_made, 1)
            nc.vector.tensor_tensor(pick[:], ident_bf[:, 32:64], ident_bf[:, 64:96], ALU.add).then_inc(spread_made, 1)
            dve.wait_ge(spread_made, 2)
            nc.vector.tensor_tensor(pick[:], pick[:], ident_bf[:, 96:128], ALU.add).then_inc(spread_made, 1)
            dve.wait_ge(spread_made, 3)
            nc.vector.tensor_copy(spread[:], pick[:].unsqueeze(2).to_broadcast([P, 2 * S, P])).then_inc(spread_made, 1)
            dve.wait_ge(weights_in, 19 * 16)
            for half in range(HALVES):
                for k in range(TAPS):
                    nc.vector.tensor_scalar(tap_w[:, half, k], in_w[:, half, :], conv_taps[:, half, k:k + 1],
                                            None, ALU.mult).then_inc(scaled_w, 1)
            nc.vector.tensor_scalar(one_minus_mu[:], mix_mu[:], -1.0, 1.0, ALU.mult, ALU.add).then_inc(scaled_w, 1)
            dve.wait_ge(a_made, 1)
            nc.vector.tensor_scalar(neg_a[:], neg_a[:], -1.0, None, ALU.mult).then_inc(a_made, 1)
            dve.wait_ge(w_transposed, 1)
            nc.vector.tensor_copy(tap_wT[:, 0], bank[0][:].rearrange("p (k d) -> p k d", d=P))
            nc.vector.tensor_copy(tap_wT[:, 1], bank[1][:].rearrange("p (k d) -> p k d", d=P))
            nc.vector.tensor_copy(z_wT[:], bank[2][:, 0:2 * P].rearrange("p (k d) -> p k d", d=P))
            nc.vector.tensor_copy(xp_wT[:], bank[2][:, 2 * P:].rearrange("p (k d) -> p k d", d=P))
            nc.vector.tensor_copy(out_wT[:], bank[3][:, 0:2 * P].rearrange("p (k d) -> p k d", d=P))
            nc.vector.tensor_copy(dt_wT[:], bank[3][0:RANK, 2 * P:].rearrange("p (k d) -> p k d", d=P))
            nc.vector.tensor_copy(mix_wT[:], bank[4][:, 0:3 * P].rearrange("p (k d) -> p k d", d=P)).then_inc(w_drained, 1)
            dve.wait_ge(w_drained, 1)
            for i in range(2):
                nc.vector.tensor_scalar(mix_now[:, i], mix_wT[:, i], mix_mu[:, i:i + 1], None, ALU.mult)
                nc.vector.tensor_scalar(mix_before[:, i], mix_wT[:, i], one_minus_mu[:, i:i + 1], None,
                                        ALU.mult).then_inc(mix_made, 1)

            def statistics(src, st, semaphore, base):
                for j in range(PT):
                    last = nc.vector.bn_stats(st["bn"][:, j, :], src[:, j, :])
                last.then_inc(semaphore, 1)
                dve.wait_ge(semaphore, base + 1)
                bn = st["bn"]
                nc.vector.tensor_tensor(st["dif"][:], bn[:, :, 1], bn[:, :, 4], ALU.subtract)
                nc.vector.tensor_tensor(st["sum2"][:], bn[:, :, 1], bn[:, :, 4], ALU.add)
                nc.vector.tensor_tensor(st["m2"][:], bn[:, :, 2], bn[:, :, 5], ALU.add).then_inc(semaphore, 1)
                dve.wait_ge(semaphore, base + 2)
                nc.vector.tensor_tensor(st["sq"][:], st["dif"][:], st["dif"][:], ALU.mult).then_inc(semaphore, 1)
                dve.wait_ge(semaphore, base + 3)
                nc.vector.scalar_tensor_tensor(out=st["var"][:], in0=st["sq"][:], scalar=P / 4.0, in1=st["m2"][:],
                                               op0=ALU.mult, op1=ALU.add).then_inc(semaphore, 1)

            def shift_of(st, scale, semaphore):
                nc.vector.scalar_tensor_tensor(out=st["shift"][:], in0=st["sum2"][:], scalar=-0.5, in1=scale[:],
                                               op0=ALU.mult, op1=ALU.mult).then_inc(semaphore, 1)

            def normalize(dst, src, scale, st):
                for j in range(PT):
                    last = nc.vector.tensor_scalar(dst[:, j, :], src[:, j, :], scale[:, j:j + 1],
                                                   st["shift"][:, j:j + 1], ALU.mult, ALU.add)
                return last

            def make_dbu(w, par, n):
                t = (w - 1) * STEPS + n
                bi = n // S
                dve.wait_ge(b_spread, t + 1)
                if n % S == 0:
                    dve.wait_ge(dtu_made, 4 * (w - 1) + 2 * bi + 2)
                wait(dve, scanned, 2 * t - 2)
                nc.vector.tensor_tensor(dbu[:, n % 2], dtu[1 - par][:, :, bi, :],
                                        b_ps[:].unsqueeze(1).to_broadcast([P, HALVES, L]),
                                        ALU.mult).then_inc(dbu_made, 1)

            def take_y(e, bi, parity, previous):
                dve.wait_ge(y_added, e * STEPS + (bi + 1) * S)
                wait(dve, filled[bank_of(previous[0])], count_of(*previous))
                for half in range(HALVES):
                    last = nc.vector.scalar_tensor_tensor(
                        out=yg[:, half], in0=xc[parity][:, half, bi, :], scalar=d_skip[:, half:half + 1],
                        in1=y_acc[half][:], op0=ALU.mult, op1=ALU.add)
                last.then_inc(y_taken, 1)

            def take_v(group, w, bi):
                b = bank_of(group)
                dve.wait_ge(filled[b], count_of(group, w))
                dve.wait_ge(filled[bank_of("back_tr1")], count_of("back_tr1", w - 1 if bi else w))
                for j in range(TILES):
                    jj = bi * TILES + j
                    last = nc.vector.scalar_tensor_tensor(
                        out=v[:, jj, :], in0=xb[:, jj, :], scalar=r1_back[:, jj:jj + 1],
                        in1=misc[b][:, j * P:(j + 1) * P], op0=ALU.mult, op1=ALU.add)
                last.then_inc(drained[b], 1)

            def body(w, par, front, scan, back):
                for n in range(STEPS):
                    if scan:
                        t = (w - 1) * STEPS + n
                        if n + 1 < STEPS:
                            make_dbu(w, par, n + 1)
                        elif front:
                            make_dbu(w + 1, 1 - par, 0)
                        wait(dve, prod_made, t - 3)
                        dve.wait_ge(dbu_made, t + 1)
                        for half in range(HALVES):
                            dve.wait_ge(da_made, 2 * t + half + 1)
                            nc.vector.tensor_tensor_scan(h[:, n % 4, half], da[half][:], dbu[:, n % 2, half], 0.0,
                                                         ALU.mult, ALU.add).then_inc(scanned, 1)
                    if n == 0 and front:
                        dve.wait_ge(xf_in, 16 * (w + 1))
                        statistics(xf, st_front, front_stat, 6 * w)
                    if n == 2 and back:
                        take_y(w - 2, 1, par, ("outproj0", w - 1))
                    if n == 2 and front:
                        dve.wait_ge(front_rstd, 4 * w + 2)
                        nc.vector.tensor_tensor(r1_sq[:], r1[par][:], r1[par][:], ALU.mult).then_inc(front_stat, 1)
                        dve.wait_ge(front_stat, 6 * w + 5)
                        nc.vector.tensor_tensor(var_u[:], r1_sq[:], st_front["var"][:], ALU.mult).then_inc(front_stat, 1)
                    if n == 4 and front:
                        dve.wait_ge(front_rstd, 4 * w + 4)
                        nc.vector.tensor_tensor(st_front["rstd"][:], r1[par][:], r2[:], ALU.mult).then_inc(front_shift, 1)
                        dve.wait_ge(front_shift, 2 * w + 1)
                        shift_of(st_front, st_front["rstd"], front_shift)
                        dve.wait_ge(front_shift, 2 * w + 2)
                        normalize(hn, xf, st_front["rstd"], st_front).then_inc(hn_made, 1)
                    if n == 5 and back:
                        take_v("outproj1", w, 1)
                    if n == 6 and back:
                        dve.wait_ge(drained[bank_of("outproj1")], count_of("outproj1", w))
                        statistics(v, st_attn, attn_stat, 4 * (w - 2))
                    if n == 8 and back:
                        dve.wait_ge(attn_rstd, 2 * (w - 1))
                        shift_of(st_attn, st_attn["rstd"], attn_shift)
                        dve.wait_ge(attn_shift, w - 1)
                        dve.wait_ge(out_made, w - 1)
                        normalize(x1, v, st_attn["rstd"], st_attn).then_inc(x1_scaled, 1)
                    if n == 10 and back:
                        dve.wait_ge(x1_made, w - 1)
                        statistics(x1, st_mid, mid_stat, 4 * (w - 2))
                    if n == 12 and back:
                        dve.wait_ge(mid_rstd, 2 * (w - 1))
                        shift_of(st_mid, st_mid["rstd"], mid_shift)
                        dve.wait_ge(mid_shift, w - 1)
                        normalize(f, x1, st_mid["rstd"], st_mid).then_inc(f_made, 1)
                    if n == 18 and scan:
                        take_y(w - 1, 0, 1 - par, ("outproj1", w))
                    if n == 20 and scan:
                        nc.vector.tensor_copy(r1_back[:], r1[1 - par][:]).then_inc(r1_kept, 1)
                    if n == 21 and front:
                        for bi in range(2):
                            g = f"xproj{bi}"
                            b = bank_of(g)
                            pt = parts[par][:, bi, :]
                            dve.wait_ge(hi_made, 2 * w + bi + 1)
                            nc.vector.tensor_tensor(rest[64:P, bi], misc[b][64:P, :], pt[64:P], ALU.subtract).then_inc(drained[b], 1)
                            dve.wait_ge(drained[b], count_of(g, w))
                            nc.vector.tensor_copy(pt[64:P], rest[64:P, bi]).then_inc(parts_made, 1)
                            dve.wait_ge(parts_made, 4 * w + 2 * bi + 1)
                            nc.vector.tensor_tensor(pt[96:P], rest[96:P, bi], pt[96:P], ALU.subtract).then_inc(parts_made, 1)
                    if n == 21 and scan:
                        dve.wait_ge(r1_kept, w)
                        dve.wait_ge(xb_in, 16 * w)
                        take_v("outproj0", w, 0)
                    if n in (23, 25) and front:
                        bi = (n - 23) // 2
                        dve.wait_ge(ln_made, 2 * w + bi + 1)
                        wait(dve, soft_made, 6 * w + 3 * bi)
                        nc.vector.tensor_scalar(soft_lin[:], soft[:, bi], 1.0, -1.0, ALU.add, ALU.add).then_inc(soft_made, 1)
                        dve.wait_ge(soft_made, 6 * w + 3 * bi + 1)
                        nc.vector.tensor_tensor(soft_ln[:], soft_ln[:], soft_lin[:], ALU.subtract).then_inc(soft_made, 1)
                        dve.wait_ge(soft_made, 6 * w + 3 * bi + 2)
                        nc.vector.scalar_tensor_tensor(out=soft[:, bi], in0=soft_ln[:], scalar=0.0,
                                                       in1=soft[:, bi], op0=ALU.min, op1=ALU.add).then_inc(soft_made, 1)
                    if n == 25 and back:
                        dve.wait_ge(out_stored, 16 * (w - 1))
                        for bi in range(2):
                            g = f"value{bi}"
                            b = bank_of(g)
                            dve.wait_ge(filled[b], count_of(g, w))
                            nc.vector.tensor_tensor(o[:, bi * TILES:(bi + 1) * TILES, :],
                                                    gate[:, bi * TILES:(bi + 1) * TILES, :],
                                                    misc[b][:].rearrange("p (j d) -> p j d", d=P),
                                                    ALU.mult).then_inc(drained[b], 1)
                        for bi in range(2):
                            g = f"value{bi}"
                            dve.wait_ge(drained[bank_of(g)], count_of(g, w))
                        statistics(o, st_out, out_stat, 4 * (w - 2))
                    if n == 28 and back:
                        dve.wait_ge(out_rstd, 2 * (w - 1))
                        shift_of(st_out, st_out["rstd"], out_shift)
                        dve.wait_ge(out_shift, w - 1)
                        normalize(o, o, st_out["rstd"], st_out).then_inc(o_scaled, 1)
                if front and not scan:
                    make_dbu(w + 1, 1 - par, 0)

            bodies(dve, body)

        @block.tensor
        def _(pe):
            pe.wait_ge(ident_made, 2)
            pe.wait_ge(weights_in, 19 * 16)
            pe.wait_ge(scaled_w, HALVES * TAPS + 1)
            tr = lambda dst, src: nc.tensor.transpose(dst, src, ident[:])
            for half in range(HALVES):
                cols = slice(half * P, (half + 1) * P)
                for k in range(TAPS):
                    tr(bank[half][:, k * P:(k + 1) * P], tap_w[:, half, k])
                tr(bank[2][:, cols], in_w[:, 2 + half, :])
                tr(bank[2][:, 2 * P + half * P:2 * P + (half + 1) * P], xp_rows[:, cols])
                tr(bank[3][:, cols], out_w[:, cols])
                tr(bank[3][0:RANK, 2 * P + half * P:2 * P + (half + 1) * P], dt_w_rows[:, half, :])
            for i in range(3):
                last = tr(bank[4][:, i * P:(i + 1) * P], mix_w[:, i, :])
            last.then_inc(w_transposed, 1)
            pe.wait_ge(w_drained, 1)
            pe.wait_ge(mix_made, 2)
            pe.wait_ge(spread_made, 4)
            pe.wait_ge(consts_made, 1)

            def bank_free(group, w):
                b = bank_of(group)
                wait(pe, drained[b], count_of(group, w) - 1)
                return misc[b]

            def done(group, last):
                last.then_inc(filled[bank_of(group)], 1)

            def skip(groups, w):
                for g in groups:
                    bank_free(g, w)
                    pe.sem_inc(filled[bank_of(g)], 1)
                    pe.sem_inc(drained[bank_of(g)], 1)

            def evacuated(group, w):
                pe.wait_ge(drained[bank_of(group)], count_of(group, w))

            def spread_b(w, par, n):
                t = (w - 1) * STEPS + n
                bi, s = n // S, n % S
                if s == 0:
                    pe.wait_ge(parts_made, 4 * (w - 1) + 2 * bi + 2)
                wait(pe, dbu_made, t)
                nc.tensor.matmul(b_ps[:], spread[:, s, :], parts[1 - par][:, bi, :],
                                 start=True, stop=True).then_inc(b_spread, 1)

            def spread_c(w, par, n):
                t = (w - 1) * STEPS + n
                bi, s = n // S, n % S
                wait(pe, c_copied, t)
                nc.tensor.matmul(c_ps[:], spread[:, S + s, :], parts[1 - par][:, bi, :],
                                 start=True, stop=True).then_inc(c_spread, 1)

            def add_states(w, n):
                t = (w - 1) * STEPS + n
                s = n % S
                if s == 0:
                    wait(pe, y_taken, 2 * (w - 1) + n // S)
                pe.wait_ge(prod_made, t + 1)
                for half in range(HALVES):
                    last = nc.tensor.matmul(y_acc[half][:], ident[:], prod[:, n % 2, half],
                                            start=(s == 0), stop=(s == S - 1))
                last.then_inc(y_added, 1)

            def transposes(group, w, src, bi):
                dst = bank_free(group, w)
                for j in range(TILES):
                    last = nc.tensor.transpose(dst[:, j * P:(j + 1) * P], src[:, bi * TILES + j, :], ident[:])
                done(group, last)

            def out_project(group, w):
                dst = bank_free(group, w)
                for j in range(TILES):
                    for half in range(HALVES):
                        last = nc.tensor.matmul(dst[:, j * P:(j + 1) * P], yg[:, half, j * P:(j + 1) * P],
                                                out_wT[:, half, :], start=(half == 0), stop=(half == HALVES - 1))
                done(group, last)

            def body(w, par, front, scan, back):
                for n in range(STEPS):
                    if scan:
                        if n + 2 < STEPS:
                            spread_b(w, par, n + 2)
                        elif front:
                            spread_b(w + 1, 1 - par, n + 2 - STEPS)
                        if n + 1 < STEPS:
                            spread_c(w, par, n + 1)
                        elif front:
                            spread_c(w + 1, 1 - par, 0)
                        if n >= LAG:
                            add_states(w, n - LAG)
                    if n < LAG and back:
                        add_states(w - 1, n - LAG + STEPS)
                    if n == 4:
                        if back:
                            pe.wait_ge(y_gated, 2 * (w - 1))
                            out_project("outproj1", w)
                        else:
                            skip(["outproj1"], w)
                    if n == 5:
                        if front:
                            pe.wait_ge(hn_made, w + 1)
                            for bi in range(2):
                                transposes(f"front_tr{bi}", w, hn, bi)
                        else:
                            skip(["front_tr0", "front_tr1"], w)
                    if 7 <= n < 11 and front:
                        bi, half = (n - 7) // 2, (n - 7) % 2
                        g = f"conv{bi}{half}"
                        if half == 0:
                            evacuated(f"front_tr{bi}", w)
                        dst = bank_free(g, w)
                        for back_by in range(TAPS):
                            last = nc.tensor.matmul(dst[:, back_by:L], tap_wT[:, half, TAPS - 1 - back_by],
                                                    hT[:, bi, 0:L - back_by], start=(back_by == 0),
                                                    stop=(back_by == TAPS - 1))
                        done(g, last)
                    if n in (11, 12) and front:
                        bi = n - 11
                        for half in range(HALVES):
                            g = f"z{bi}{half}"
                            done(g, nc.tensor.matmul(bank_free(g, w)[:], z_wT[:, half], hT[:, bi, :],
                                                     start=True, stop=True))
                    if n == 12 and not front:
                        skip([f"{a}{bi}{half}" for a in ("conv", "z") for bi in range(2) for half in range(2)], w)
                    if n == 13:
                        if back:
                            pe.wait_ge(f_made, w - 1)
                            for bi in range(2):
                                transposes(f"back_tr{bi}", w, f, bi)
                        else:
                            skip(["back_tr0", "back_tr1"], w)
                    if n == 15:
                        if back:
                            for bi in range(2):
                                g = f"key{bi}"
                                evacuated(f"back_tr{bi}", w)
                                dst = bank_free(g, w)
                                nc.tensor.matmul(dst[:], mix_now[:, 1], fT[:, bi, 1:L + 1], start=True, stop=False)
                                done(g, nc.tensor.matmul(dst[:], mix_before[:, 1], fT[:, bi, 0:L],
                                                         start=False, stop=True))
                        else:
                            skip(["key0", "key1"], w)
                    if n == 16:
                        if back:
                            for bi in range(2):
                                g = f"gate{bi}"
                                dst = bank_free(g, w)
                                for j in range(TILES):
                                    nc.tensor.matmul(dst[:, j * P:(j + 1) * P], fT[:, bi, j * P + 1:(j + 1) * P + 1],
                                                     mix_now[:, 0], start=True, stop=False)
                                    last = nc.tensor.matmul(dst[:, j * P:(j + 1) * P], fT[:, bi, j * P:(j + 1) * P],
                                                            mix_before[:, 0], start=False, stop=True)
                                done(g, last)
                        else:
                            skip(["gate0", "gate1"], w)
                    if n == 19:
                        if front:
                            pe.wait_ge(silu_made, 2 * w + 1)
                            for bi in range(2):
                                g = f"xproj{bi}"
                                dst = bank_free(g, w)
                                for half in range(HALVES):
                                    last = nc.tensor.matmul(dst[:], xp_wT[:, half], xc[par][:, half, bi, :],
                                                            start=(half == 0), stop=(half == HALVES - 1))
                                done(g, last)
                        else:
                            skip(["xproj0", "xproj1"], w)
                    if n == 20:
                        if scan:
                            pe.wait_ge(y_gated, 2 * (w - 1) + 1)
                            out_project("outproj0", w)
                        else:
                            skip(["outproj0"], w)
                    if n in (21, 23):
                        bi = (n - 21) // 2
                        if front:
                            pe.wait_ge(hi_made, 2 * w + bi + 1)
                            for half in range(HALVES):
                                g = f"dt{bi}{half}"
                                done(g, nc.tensor.matmul(bank_free(g, w)[:], dt_wT[:, half], dt_low[:, bi, :],
                                                         start=True, stop=True))
                        else:
                            skip([f"dt{bi}0", f"dt{bi}1"], w)
                    if n == 24:
                        if back:
                            pe.wait_ge(key_squared, w - 1)
                            for bi in range(2):
                                g = f"value{bi}"
                                dst = bank_free(g, w)
                                for j in range(TILES):
                                    last = nc.tensor.matmul(dst[:, j * P:(j + 1) * P], key[:, bi, j * P:(j + 1) * P],
                                                            mix_wT[:, 2], start=True, stop=True)
                                done(g, last)
                        else:
                            skip(["value0", "value1"], w)
                if front and not scan:
                    spread_b(w + 1, 1 - par, 0)
                    spread_c(w + 1, 1 - par, 0)
                    spread_b(w + 1, 1 - par, 1)

            bodies(pe, body)


_INS = ["L0_attn_x", "L0_attn_ln_gamma", "L0_attn_ln_beta", "L0_attn_in_proj_w", "L0_attn_conv_w",
        "L0_attn_conv_b", "L0_attn_x_proj_w", "L0_attn_dt_proj_w", "L0_attn_dt_proj_b", "L0_attn_A_log",
        "L0_attn_D", "L0_attn_out_proj_w", "L0_ffn_W_r", "L0_ffn_W_k", "L0_ffn_W_v", "L0_ffn_mu_r",
        "L0_ffn_mu_k"]


def kernel(**inputs):
    import numpy as np
    import concourse.bacc as bacc
    from concourse import mybir as _mybir
    from concourse.bass_utils import run_bass_kernel_spmd

    nc = bacc.Bacc("TRN2", target_bir_lowering=False, num_devices=1)
    arrays, args = {}, []
    for name in _INS:
        a = np.ascontiguousarray(inputs[name])
        arrays[f"in_{name}"] = a
        args.append(nc.dram_tensor(f"in_{name}", a.shape, _mybir.dt.from_np(a.dtype), kind="ExternalInput").ap())
    shape = inputs["L0_attn_x"].shape
    args.append(nc.dram_tensor("out", shape, _mybir.dt.float32, kind="ExternalOutput").ap())
    mamba_sandwich(nc, *args)
    r = run_bass_kernel_spmd(nc, [arrays], core_ids=[0])
    return r.results[0]["out"]
```

```python
from contextlib import ExitStack

import concourse.bass as bass
from concourse import mybir

FP32 = mybir.dt.float32
BF16 = mybir.dt.bfloat16
ALU = mybir.AluOpType
ACT = mybir.ActivationFunctionType

EPS = 1e-5
EXP_LN_SET = "natural_log_exp_and_others"
P = 128
L = 512
S = 16
HALVES = 2
TAPS = 4
RANK = 8
TILES = L // P
PT = 2 * TILES
STEPS = 2 * S
LAG = 3
B_AHEAD = 3
DBU_AHEAD = 2
POOL_AHEAD = 4
RING = 4
POOL_STEPS = (3, 7, 11, 14, 18, 22, 25, 28)

GROUPS = ["front_tr0", "front_tr1", "outproj1", "conv00", "conv01", "conv10", "conv11",
          "z00", "z01", "z10", "z11", "back_tr0", "back_tr1", "key0", "key1", "gate0", "gate1",
          "xproj0", "outproj0", "xproj1", "dt00", "dt01", "value0", "value1", "dt10", "dt11"]
PER_BANK = len(GROUPS) // 2


def bank_of(group):
    return GROUPS.index(group) % 2


def count_of(group, w):
    return w * PER_BANK + (GROUPS.index(group) // 2 + 1)


def by_pool(n):
    return n % STEPS in POOL_STEPS


def pool_made(pair, n):
    return pair * len(POOL_STEPS) + sum(by_pool(i) for i in range(n))


def dve_made(pair, n):
    return pair * (STEPS - len(POOL_STEPS)) + sum(not by_pool(i) for i in range(n))


def wait(engine, semaphore, value):
    if not isinstance(value, int) or value > 0:
        engine.wait_ge(semaphore, value)


def mamba_sandwich(nc, x, ln_gamma, ln_beta, in_proj_w, conv_w, conv_b, x_proj_w, dt_proj_w,
                   dt_proj_b, A_log, D, out_proj_w, W_r, W_k, W_v, mu_r, mu_k, out):
    pairs = x.shape[0] // 2
    x_pairs = x.rearrange("(w b) (j p) d -> w p (b j) d", b=2, p=P)
    out_pairs = out.rearrange("(w b) (j p) d -> w p (b j) d", b=2, p=P)

    ctx = ExitStack()
    with ctx:
        def sb(name, shape, dt=FP32):
            return ctx.enter_context(nc.sbuf_tensor(name, shape, dt))

        def sem(name):
            return ctx.enter_context(nc.semaphore(name))

        h = sb("h", [P, RING, HALVES, L])
        staged = h[:].rearrange("p a b (c d) -> p (a b c) d", d=P)
        in_w = staged[:, 0:4]
        conv_taps = sb("conv_taps", [P, HALVES, TAPS])
        conv_bias = sb("conv_bias", [P, HALVES])
        xp_rows = staged[:, 4:6].rearrange("p a d -> p (a d)")
        dt_w_rows = sb("dt_w_rows", [P, HALVES, RANK])
        dt_bias = sb("dt_bias", [P, HALVES])
        a_log = sb("a_log", [P, HALVES, S])
        d_skip = sb("d_skip", [P, HALVES])
        out_w = staged[:, 6:8].rearrange("p a d -> p (a d)")
        mix_w = staged[:, 8:11]
        mix_mu = sb("mix_mu", [P, 2])
        gamma_beta = sb("gamma_beta", [P, 2])

        ident = sb("ident", [P, P])
        ident_bf = sb("ident_bf", [P, P], BF16)
        pick = sb("pick", [P, 2 * S], BF16)
        spread = sb("spread", [P, 2 * S, P], BF16)
        eps_col = sb("eps_col", [P, 1])
        eps_sq_col = sb("eps_sq_col", [P, 1])
        one_col = sb("one_col", [P, 1])
        tap_wT = sb("tap_wT", [P, HALVES, TAPS, P])
        z_wT = sb("z_wT", [P, HALVES, P])
        xp_wT = sb("xp_wT", [P, HALVES, P])
        dt_wT = sb("dt_wT", [RANK, HALVES, P])
        neg_a = sb("neg_a", [P, HALVES, S])
        out_wT = sb("out_wT", [P, HALVES, P])
        mix_wT = sb("mix_wT", [P, 3, P])
        one_minus_mu = sb("one_minus_mu", [P, 2])
        mix_now = sb("mix_now", [P, 2, P])
        mix_before = sb("mix_before", [P, 2, P])

        xf = sb("xf", [P, PT, P])
        hn = sb("hn", [P, PT, P])
        tap_w = hn[:].rearrange("p (h k) d -> p h k d", h=HALVES)
        hT = sb("hT", [P, 2, L])
        xc = [sb(f"xc{i}", [P, HALVES, 2, L]) for i in range(2)]
        zs = [sb(f"zs{i}", [P, HALVES, 2, L]) for i in range(2)]
        dt = [sb(f"dt{i}", [P, HALVES, 2, L]) for i in range(2)]
        dtu = [sb(f"dtu{i}", [P, HALVES, 2, L]) for i in range(2)]
        parts = [sb(f"parts{i}", [P, 2, L], BF16) for i in range(2)]
        low_rest = sb("low_rest", [P, 2, L])
        dt_low = low_rest[0:RANK]
        rest = low_rest[:, 0]
        soft = sb("soft", [P, 2, HALVES, L])
        soft_ln = hn[:].rearrange("p (a t) d -> p a (t d)", a=HALVES)
        soft_lin = hT

        dbu = sb("dbu", [P, RING, HALVES, L])
        b_sb = sb("b_sb", [P, 2, L])
        c_sb = sb("c_sb", [P, RING, L])
        prod = sb("prod", [P, RING, HALVES, L])

        xb = sb("xb", [P, PT, P])
        yg = sb("yg", [P, HALVES, L])
        v = sb("v", [P, PT, P])
        x1 = sb("x1", [P, PT, P])
        f = v
        fT = sb("fT", [P, 2, L + 1])
        key = sb("key", [P, 2, L])
        o = sb("o", [P, PT, P])
        gate = o

        def stat_tiles(name):
            return {k: sb(f"{name}_{k}", [P, PT] + ([6] if k == "bn" else []))
                    for k in ("bn", "sum2", "dif", "m2", "sq", "var", "ln", "rstd", "shift")}

        st_front, st_attn, st_mid, st_out = (stat_tiles(n) for n in ("front", "attn", "mid", "out"))
        front_ln = sb("front_ln2", [P, 2, PT])
        front_rstds = [sb(f"front_rstds{i}", [P, 2, PT]) for i in range(2)]
        r1_back = sb("r1_back", [P, PT])

        bank = [ctx.enter_context(nc.psum_tensor(f"bank{i}", [P, L], FP32)) for i in range(8)]
        misc, da, y_acc, b_ps, c_ps = bank[0:2], bank[2:4], bank[4:6], bank[6], bank[7]

        weights_in, weights_cleared = sem("weights_in"), sem("weights_cleared")
        ident_made, consts_made, scaled_w = sem("ident_made"), sem("consts_made"), sem("scaled_w")
        w_transposed, w_drained, a_made = sem("w_transposed"), sem("w_drained"), sem("a_made")
        spread_made, mix_made = sem("spread_made"), sem("mix_made")
        filled = [sem("misc_filled0"), sem("misc_filled1")]
        drained = [sem("misc_drained0"), sem("misc_drained1")]
        xf_in, xb_in, out_stored = sem("xf_in"), sem("xb_in"), sem("out_stored")
        front_stat, front_rstd, hn_made = sem("front_stat"), sem("front_rstd"), sem("hn_made")
        silu_made, key_squared, soft_exp, ln_made = sem("silu_made"), sem("key_squared"), sem("soft_exp"), sem("ln_made")
        hi_made, parts_made, soft_made = sem("hi_made"), sem("parts_made"), sem("soft_made")
        dt_dve, dt_pool = sem("dt_dve"), sem("dt_pool")
        b_spread, b_copied, c_spread, c_copied = sem("b_spread"), sem("b_copied"), sem("c_spread"), sem("c_copied")
        da_made, dbu_dve, dbu_pool, scanned = sem("da_made"), sem("dbu_dve"), sem("dbu_pool"), sem("scanned")
        prod_made, y_added = sem("prod_made"), sem("y_added")
        y_taken, y_gated, r1_kept, v_made = sem("y_taken"), sem("y_gated"), sem("r1_kept"), sem("v_made")
        attn_stat, attn_rstd, x1_scaled, x1_made = sem("attn_stat"), sem("attn_rstd"), sem("x1_scaled"), sem("x1_made")
        mid_stat, mid_rstd, f_made = sem("mid_stat"), sem("mid_rstd"), sem("f_made")
        out_stat, out_rstd, o_scaled, out_made = sem("out_stat"), sem("out_rstd"), sem("o_scaled"), sem("out_made")
        front_shift, attn_shift, mid_shift, out_shift = (sem(f"{n}_shift") for n in ("front", "attn", "mid", "out"))

        def bodies(engine, body):
            body(0, 0, front=True, scan=False, back=False)
            body(1, 1, front=True, scan=True, back=False)
            with engine.Fori(2, pairs, 2) as w:
                body(w, 0, front=True, scan=True, back=True)
                body(w + 1, 1, front=True, scan=True, back=True)
            body(pairs, 0, front=False, scan=True, back=True)
            body(pairs + 1, 1, front=False, scan=False, back=True)

        block = ctx.enter_context(nc.Block())

        @block.sync
        def _(sp):
            
            def load_column(dst, vector):
                sp.dma_start(dst, vector.rearrange("(h p) -> p h", p=P),
                             allow_slow_non_contiguous=True).then_inc(weights_in, 16)

            sp.dma_start(xf[:], x_pairs[0]).then_inc(xf_in, 16)
            sp.sem_inc(out_stored, 16)
            sp.dma_start(in_w, in_proj_w.rearrange("(c p) d -> p c d", p=P)).then_inc(weights_in, 16)
            sp.dma_start(conv_taps[:], conv_w.rearrange("(h p) k -> p h k", p=P)).then_inc(weights_in, 16)
            load_column(conv_bias[:], conv_b)
            sp.dma_start(dt_w_rows[:], dt_proj_w.rearrange("(h p) r -> p h r", p=P)).then_inc(weights_in, 16)
            load_column(dt_bias[:], dt_proj_b)
            sp.dma_start(a_log[:], A_log.rearrange("(h p) s -> p h s", p=P)).then_inc(weights_in, 16)
            load_column(d_skip[:], D)
            sp.dma_start(out_w, out_proj_w).then_inc(weights_in, 16)
            for i, wt in enumerate((W_r, W_k, W_v)):
                sp.dma_start(mix_w[:, i, :], wt).then_inc(weights_in, 16)
            for i, mu in enumerate((mu_r, mu_k)):
                load_column(mix_mu[:, i:i + 1], mu)
            for i, g in enumerate((ln_gamma, ln_beta)):
                load_column(gamma_beta[:, i:i + 1], g)
            sp.wait_ge(weights_cleared, 1)
            sp.dma_start(xp_rows[0:RANK, :], x_proj_w[0:RANK, :]).then_inc(weights_in, 16)
            for i in range(1, 4):
                sp.dma_start(xp_rows[32 * i:32 * i + 2 * S, :],
                             x_proj_w[RANK:RANK + 2 * S, :]).then_inc(weights_in, 16)

            def body(w, par, front, scan, back):
                if front and not (isinstance(w, int) and w >= pairs - 1):
                    sp.wait_ge(hn_made, 2 * w + 2)
                    sp.dma_start(xf[:], x_pairs[w + 1]).then_inc(xf_in, 16)
                if scan:
                    wait(sp, x1_made, w - 1)
                    sp.dma_start(xb[:], x_pairs[w - 1]).then_inc(xb_in, 16)
                if back:
                    sp.wait_ge(out_made, w)
                    sp.dma_start(out_pairs[w - 2], o[:]).then_inc(out_stored, 16)

            body(0, 0, True, False, False)
            body(1, 1, True, True, False)
            with sp.Fori(2, pairs - 2, 2) as w:
                body(w, 0, True, True, True)
                body(w + 1, 1, True, True, True)
            body(pairs - 2, 0, True, True, True)
            body(pairs - 1, 1, True, True, True)
            body(pairs, 0, False, True, True)
            body(pairs + 1, 1, False, False, True)
            sp.wait_ge(out_stored, 16 * (pairs + 1))

        @block.gpsimd
        def _(pool):
            nc.gpsimd.memset(ident[:], 0.0).then_inc(ident_made, 1)
            pool.wait_ge(ident_made, 1)
            nc.gpsimd.affine_select(out=ident[:], in_=ident[:], compare_op=ALU.not_equal, fill=1.0,
                                    base=0, pattern=[[-1, P]], channel_multiplier=1).then_inc(ident_made, 1)
            pool.sem_inc(out_made, 1)

            def make_dbu(pair, par, n):
                if not by_pool(n):
                    return
                bi = n // S
                pool.wait_ge(b_copied, pool_made(pair, n) + 1)
                pool.wait_ge((dt_dve, dt_pool)[bi], 2 * pair + 2)
                wait(pool, scanned, 2 * (pair * STEPS + n + 1 - RING))
                nc.gpsimd.tensor_tensor(dbu[:, n % RING], dtu[par][:, :, bi, :],
                                        b_sb[:, sum(by_pool(i) for i in range(n)) % 2].unsqueeze(1).to_broadcast([P, HALVES, L]),
                                        ALU.mult).then_inc(dbu_pool, 1)

            def body(w, par, front, scan, back):
                for n in range(STEPS):
                    if scan:
                        t = (w - 1) * STEPS + n
                        pool.wait_ge(scanned, 2 * t + 2)
                        pool.wait_ge(c_copied, t + 1)
                        wait(pool, y_added, t + 1 - RING)
                        nc.gpsimd.tensor_tensor(
                            prod[:, n % RING], h[:, n % RING],
                            c_sb[:, n % RING].unsqueeze(1).to_broadcast([P, HALVES, L]),
                            ALU.mult).then_inc(prod_made, 1)
                        if n + POOL_AHEAD < STEPS:
                            make_dbu(w - 1, 1 - par, n + POOL_AHEAD)
                        elif front:
                            make_dbu(w, par, n + POOL_AHEAD - STEPS)
                    if n == 3 and scan:
                        pool.wait_ge(soft_made, 6 * w)
                        nc.gpsimd.tensor_tensor(dt[1 - par][:, :, 1, :], dt[1 - par][:, :, 1, :], soft[:, 1],
                                                ALU.add).then_inc(dt_pool, 1)
                    if n == 5 and scan:
                        pool.wait_ge(dt_pool, 2 * w - 1)
                        nc.gpsimd.tensor_tensor(dtu[1 - par][:, :, 1, :], dt[1 - par][:, :, 1, :],
                                                xc[1 - par][:, :, 1, :], ALU.mult).then_inc(dt_pool, 1)
                    if n == 31 and back:
                        pool.wait_ge(o_scaled, 2 * (w - 1))
                        nc.gpsimd.tensor_tensor(o[:], o[:], x1[:], ALU.add).then_inc(out_made, 1)
                if front and not scan:
                    for n in range(POOL_AHEAD):
                        make_dbu(w, par, n)

            bodies(pool, body)

        @block.scalar
        def _(act):
            nc.scalar.preload_act_table_set(EXP_LN_SET)
            act.wait_ge(consts_made, 1)
            act.wait_ge(weights_in, 19 * 16)
            nc.scalar.activation(neg_a[:], a_log[:], ACT.Exp).then_inc(a_made, 1)

            def rstd(out_, ln_, var_, semaphore, base, step):
                if step == 0:
                    nc.scalar.activation(ln_[:], var_[:], ACT.Ln, bias=eps_col[:], scale=1.0 / P).then_inc(semaphore, 1)
                else:
                    act.wait_ge(semaphore, base + 1)
                    nc.scalar.activation(out_[:], ln_[:], ACT.Exp, scale=-0.5).then_inc(semaphore, 1)

            def evacuate(group, w, out_, func, **kw):
                b = bank_of(group)
                act.wait_ge(filled[b], count_of(group, w))
                nc.scalar.activation(out_, misc[b][:], func, **kw).then_inc(drained[b], 1)

            def copy_b(pair, n):
                if not by_pool(n):
                    return
                act.wait_ge(b_spread, pair * STEPS + n + 1)
                wait(act, dbu_pool, pool_made(pair, n) - 1)
                nc.scalar.activation(b_sb[:, sum(by_pool(i) for i in range(n)) % 2], b_ps[:], ACT.Copy).then_inc(b_copied, 1)

            def side_work(w, par, front, scan, back, n, slot):
                if n == 2 and front:
                    if slot == 0:
                        act.wait_ge(front_stat, 4 * w + 4)
                        nc.scalar.activation(front_ln[:, 0], st_front["var"][:], ACT.Ln, bias=eps_col[:], scale=1.0 / P)
                        nc.scalar.activation(front_ln[:, 1], st_front["var"][:], ACT.Ln, bias=eps_sq_col[:],
                                             scale=(1.0 + EPS) / P).then_inc(front_rstd, 1)
                    else:
                        act.wait_ge(front_rstd, 2 * w + 1)
                        nc.scalar.activation(front_rstds[par][:], front_ln[:], ACT.Exp, scale=-0.5).then_inc(front_rstd, 1)
                if n == 5 and front:
                    evacuate(f"front_tr{slot}", w, hT[:, slot, :], ACT.Identity,
                             bias=gamma_beta[:, 1:2], scale=gamma_beta[:, 0:1])
                if n == 9 and back:
                    if slot == 0:
                        act.wait_ge(attn_stat, 4 * (w - 1))
                    rstd(st_attn["rstd"], st_attn["ln"], st_attn["var"], attn_rstd, 2 * (w - 2), slot)
                if n in (8, 10, 12, 14) and slot == 0 and front:
                    bi, half = (n - 8) // 4, (n - 8) // 2 % 2
                    if n == 8:
                        wait(act, y_taken, 2 * (w - 1))
                    evacuate(f"conv{bi}{half}", w, xc[par][:, half, bi, :], ACT.Identity,
                             bias=conv_bias[:, half:half + 1])
                if n == 13 and back:
                    if slot == 0:
                        act.wait_ge(mid_stat, 4 * (w - 1))
                    rstd(st_mid["rstd"], st_mid["ln"], st_mid["var"], mid_rstd, 2 * (w - 2), slot)
                if n in (15, 16) and front:
                    bi = n - 15
                    if bi == 0 and slot == 0:
                        wait(act, y_gated, 2 * (w - 1))
                    evacuate(f"z{bi}{slot}", w, zs[par][:, slot, bi, :], ACT.Identity)
                if n == 17 and back:
                    evacuate(f"back_tr{slot}", w, fT[:, slot, 1:L + 1], ACT.Identity)
                if (n, slot) in ((18, 1), (19, 0)) and back:
                    bi = n - 18
                    evacuate(f"key{bi}", w, key[:, bi, :], ACT.Relu)
                if (n, slot) == (20, 1) and back:
                    for bi in range(2):
                        act.wait_ge(drained[bank_of(f"key{bi}")], count_of(f"key{bi}", w))
                    nc.scalar.activation(key[:], key[:], ACT.Square).then_inc(key_squared, 1)
                if (n, slot) == (19, 1):
                    if back:
                        act.wait_ge(out_stored, 16 * (w - 1))
                        for bi in range(2):
                            evacuate(f"gate{bi}", w, gate[:, bi * TILES:(bi + 1) * TILES, :], ACT.Tanh, scale=0.5)
                    if front:
                        for g in ("z10", "z11"):
                            act.wait_ge(drained[bank_of(g)], count_of(g, w))
                        nc.scalar.activation(xc[par][:], xc[par][:], ACT.Silu).then_inc(silu_made, 1)
                        nc.scalar.activation(zs[par][:], zs[par][:], ACT.Silu).then_inc(silu_made, 1)
                    nc.scalar.preload_act_table_set(EXP_LN_SET)
                if n in (22, 23) and slot == 1 and front:
                    bi = n - 22
                    b = bank_of(f"xproj{bi}")
                    act.wait_ge(filled[b], count_of(f"xproj{bi}", w))
                    nc.scalar.activation(dt_low[:, bi, :], misc[b][0:RANK, :], ACT.Copy)
                    nc.scalar.activation(parts[par][:, bi, :], misc[b][:], ACT.Copy).then_inc(hi_made, 1)
                if n in (24, 28) and front:
                    bi, half = (n - 24) // 4, slot
                    b = bank_of(f"dt{bi}{half}")
                    act.wait_ge(filled[b], count_of(f"dt{bi}{half}", w))
                    nc.scalar.activation(soft[:, bi, half], misc[b][:], ACT.Abs, bias=dt_bias[:, half:half + 1])
                    nc.scalar.activation(dt[par][:, half, bi, :], misc[b][:], ACT.Relu,
                                         bias=dt_bias[:, half:half + 1]).then_inc(drained[b], 1)
                if n in (25, 29) and front:
                    bi = (n - 25) // 4
                    if slot == 0:
                        for half in range(HALVES):
                            act.wait_ge(drained[bank_of(f"dt{bi}{half}")], count_of(f"dt{bi}{half}", w))
                        nc.scalar.activation(soft[:, bi], soft[:, bi], ACT.Exp, scale=-1.0).then_inc(soft_exp, 1)
                    else:
                        act.wait_ge(soft_exp, 2 * w + bi + 1)
                        wait(act, soft_made, 6 * w + 3 * bi)
                        nc.scalar.activation(soft_ln, soft[:, bi], ACT.Ln, bias=one_col[:]).then_inc(ln_made, 1)
                if n == 30 and back:
                    if slot == 0:
                        act.wait_ge(out_stat, 4 * (w - 1))
                    rstd(st_out["rstd"], st_out["ln"], st_out["var"], out_rstd, 2 * (w - 2), slot)

            def body(w, par, front, scan, back):
                for n in range(STEPS):
                    for half in range(HALVES):
                        if scan:
                            t = (w - 1) * STEPS + n
                            bi, s = n // S, n % S
                            if s == 0 and half == 0:
                                act.wait_ge((dt_dve, dt_pool)[bi], 2 * w - 1)
                            wait(act, scanned, 2 * t - 1 + half)
                            nc.scalar.activation(da[half][:], dt[1 - par][:, half, bi, :], ACT.Exp,
                                                 scale=neg_a[:, half, s:s + 1]).then_inc(da_made, 1)
                            if half == 0:
                                act.wait_ge(c_spread, t + 1)
                                wait(act, prod_made, t + 1 - RING)
                                nc.scalar.activation(c_sb[:, n % RING], c_ps[:], ACT.Copy).then_inc(c_copied, 1)
                            elif n + B_AHEAD < STEPS:
                                copy_b(w - 1, n + B_AHEAD)
                            elif front:
                                copy_b(w, n + B_AHEAD - STEPS)
                        side_work(w, par, front, scan, back, n, half)
                if front and not scan:
                    for n in range(B_AHEAD):
                        copy_b(w, n)

            bodies(act, body)

        @block.vector
        def _(dve):
            nc.vector.memset(xp_rows, 0.0).then_inc(weights_cleared, 1)
            nc.vector.memset(eps_col[:], EPS)
            nc.vector.memset(eps_sq_col[:], EPS * EPS)
            nc.vector.memset(one_col[:], 1.0)
            nc.vector.memset(fT[:, :, 0:1], 0.0).then_inc(consts_made, 1)
            dve.wait_ge(ident_made, 2)
            nc.vector.tensor_copy(ident_bf[:], ident[:]).then_inc(spread_made, 1)
            dve.wait_ge(spread_made, 1)
            nc.vector.tensor_tensor(pick[:], ident_bf[:, 32:64], ident_bf[:, 64:96], ALU.add).then_inc(spread_made, 1)
            dve.wait_ge(spread_made, 2)
            nc.vector.tensor_tensor(pick[:], pick[:], ident_bf[:, 96:128], ALU.add).then_inc(spread_made, 1)
            dve.wait_ge(spread_made, 3)
            nc.vector.tensor_copy(spread[:], pick[:].unsqueeze(2).to_broadcast([P, 2 * S, P])).then_inc(spread_made, 1)
            dve.wait_ge(weights_in, 19 * 16)
            for half in range(HALVES):
                for k in range(TAPS):
                    nc.vector.tensor_scalar(tap_w[:, half, k], in_w[:, half, :], conv_taps[:, half, k:k + 1],
                                            None, ALU.mult).then_inc(scaled_w, 1)
            nc.vector.tensor_scalar(one_minus_mu[:], mix_mu[:], -1.0, 1.0, ALU.mult, ALU.add).then_inc(scaled_w, 1)
            dve.wait_ge(a_made, 1)
            nc.vector.tensor_scalar(neg_a[:], neg_a[:], -1.0, None, ALU.mult).then_inc(a_made, 1)
            dve.wait_ge(w_transposed, 1)
            nc.vector.tensor_copy(tap_wT[:, 0], bank[0][:].rearrange("p (k d) -> p k d", d=P))
            nc.vector.tensor_copy(tap_wT[:, 1], bank[1][:].rearrange("p (k d) -> p k d", d=P))
            nc.vector.tensor_copy(z_wT[:], bank[2][:, 0:2 * P].rearrange("p (k d) -> p k d", d=P))
            nc.vector.tensor_copy(xp_wT[:], bank[2][:, 2 * P:].rearrange("p (k d) -> p k d", d=P))
            nc.vector.tensor_copy(out_wT[:], bank[3][:, 0:2 * P].rearrange("p (k d) -> p k d", d=P))
            nc.vector.tensor_copy(dt_wT[:], bank[3][0:RANK, 2 * P:].rearrange("p (k d) -> p k d", d=P))
            nc.vector.tensor_copy(mix_wT[:], bank[4][:, 0:3 * P].rearrange("p (k d) -> p k d", d=P)).then_inc(w_drained, 1)
            dve.wait_ge(w_drained, 1)
            for i in range(2):
                nc.vector.tensor_scalar(mix_now[:, i], mix_wT[:, i], mix_mu[:, i:i + 1], None, ALU.mult)
                nc.vector.tensor_scalar(mix_before[:, i], mix_wT[:, i], one_minus_mu[:, i:i + 1], None,
                                        ALU.mult).then_inc(mix_made, 1)

            nc.vector.tensor_scalar(mix_wT[:, 2], mix_wT[:, 2], 0.5, None, ALU.mult).then_inc(mix_made, 1)

            def statistics(src, st, semaphore, base, step):
                bn = st["bn"]
                if step < 2:
                    for j in range(step * TILES, (step + 1) * TILES):
                        last = nc.vector.bn_stats(bn[:, j, :], src[:, j, :])
                    if step == 1:
                        last.then_inc(semaphore, 1)
                    return
                dve.wait_ge(semaphore, base + step - 1)
                if step == 2:
                    nc.vector.tensor_tensor(st["dif"][:], bn[:, :, 1], bn[:, :, 4], ALU.subtract)
                    nc.vector.tensor_tensor(st["sum2"][:], bn[:, :, 1], bn[:, :, 4], ALU.add)
                    nc.vector.tensor_tensor(st["m2"][:], bn[:, :, 2], bn[:, :, 5], ALU.add).then_inc(semaphore, 1)
                elif step == 3:
                    nc.vector.tensor_tensor(st["sq"][:], st["dif"][:], st["dif"][:], ALU.mult).then_inc(semaphore, 1)
                else:
                    nc.vector.scalar_tensor_tensor(out=st["var"][:], in0=st["sq"][:], scalar=P / 4.0, in1=st["m2"][:],
                                                   op0=ALU.mult, op1=ALU.add).then_inc(semaphore, 1)

            def shift_of(st, scale, semaphore):
                nc.vector.scalar_tensor_tensor(out=st["shift"][:], in0=st["sum2"][:], scalar=-0.5, in1=scale,
                                               op0=ALU.mult, op1=ALU.mult).then_inc(semaphore, 1)

            def normalize(dst, src, scale, st, bi, semaphore):
                for j in range(bi * TILES, (bi + 1) * TILES):
                    last = nc.vector.tensor_scalar(dst[:, j, :], src[:, j, :], scale[:, j:j + 1],
                                                   st["shift"][:, j:j + 1], ALU.mult, ALU.add)
                last.then_inc(semaphore, 1)

            def make_dbu(pair, par, n):
                if by_pool(n):
                    return
                t = pair * STEPS + n
                bi = n // S
                dve.wait_ge(b_spread, t + 1)
                if n % S == 0:
                    dve.wait_ge((dt_dve, dt_pool)[bi], 2 * pair + 2)
                wait(dve, scanned, 2 * (t + 1 - RING))
                nc.vector.tensor_tensor(dbu[:, n % RING], dtu[par][:, :, bi, :],
                                        b_ps[:].unsqueeze(1).to_broadcast([P, HALVES, L]),
                                        ALU.mult).then_inc(dbu_dve, 1)

            def take_y(e, bi, parity, previous, half):
                if half == 0:
                    dve.wait_ge(y_added, e * STEPS + (bi + 1) * S)
                    wait(dve, filled[bank_of(previous[0])], count_of(*previous))
                last = nc.vector.scalar_tensor_tensor(
                    out=yg[:, half], in0=xc[parity][:, half, bi, :], scalar=d_skip[:, half:half + 1],
                    in1=y_acc[half][:], op0=ALU.mult, op1=ALU.add)
                if half == HALVES - 1:
                    last.then_inc(y_taken, 1)

            def gate_y(e, bi, parity):
                dve.wait_ge(y_taken, 2 * e + bi + 1)
                nc.vector.tensor_tensor(yg[:], yg[:], zs[parity][:, :, bi, :], ALU.mult).then_inc(y_gated, 1)

            def take_v(group, w, bi):
                b = bank_of(group)
                dve.wait_ge(filled[b], count_of(group, w))
                dve.wait_ge(filled[bank_of("back_tr1")], count_of("back_tr1", w - 1 if bi else w))
                for j in range(TILES):
                    jj = bi * TILES + j
                    last = nc.vector.scalar_tensor_tensor(
                        out=v[:, jj, :], in0=xb[:, jj, :], scalar=r1_back[:, jj:jj + 1],
                        in1=misc[b][:, j * P:(j + 1) * P], op0=ALU.mult, op1=ALU.add)
                last.then_inc(drained[b], 1)

            def side_work(w, par, front, scan, back, n, slot):
                q = 3 * n + slot
                if q < 5 and front:
                    if q == 0:
                        dve.wait_ge(xf_in, 16 * (w + 1))
                    statistics(xf, st_front, front_stat, 4 * w, q)
                if q == 9 and front:
                    dve.wait_ge(front_rstd, 2 * w + 2)
                    shift_of(st_front, front_rstds[par][:, 1], front_shift)
                if q in (10, 11) and front:
                    dve.wait_ge(front_shift, w + 1)
                    normalize(hn, xf, front_rstds[par][:, 1], st_front, q - 10, hn_made)
                if n in (23, 24) and front:
                    bi = n - 23
                    b = bank_of(f"xproj{bi}")
                    pt = parts[par][:, bi, :]
                    if slot == 0:
                        dve.wait_ge(hi_made, 2 * w + bi + 1)
                        wait(dve, parts_made, 4 * w + 2 * bi)
                        nc.vector.tensor_tensor(rest[64:P], misc[b][64:P, :], pt[64:P], ALU.subtract).then_inc(drained[b], 1)
                    elif slot == 1:
                        dve.wait_ge(drained[b], count_of(f"xproj{bi}", w))
                        nc.vector.tensor_copy(pt[64:P], rest[64:P]).then_inc(parts_made, 1)
                    else:
                        dve.wait_ge(parts_made, 4 * w + 2 * bi + 1)
                        nc.vector.tensor_tensor(pt[96:P], rest[96:P], pt[96:P], ALU.subtract).then_inc(parts_made, 1)
                if n in (26, 30) and front:
                    bi = (n - 26) // 4
                    if slot == 0:
                        dve.wait_ge(soft_exp, 2 * w + bi + 1)
                        wait(dve, soft_made, 6 * w + 3 * bi)
                        nc.vector.tensor_scalar(soft_lin[:], soft[:, bi], 1.0, -1.0, ALU.add, ALU.add).then_inc(soft_made, 1)
                    elif slot == 1:
                        dve.wait_ge(ln_made, 2 * w + bi + 1)
                        dve.wait_ge(soft_made, 6 * w + 3 * bi + 1)
                        nc.vector.tensor_tensor(soft_ln, soft_ln, soft_lin[:], ALU.subtract).then_inc(soft_made, 1)
                    else:
                        dve.wait_ge(soft_made, 6 * w + 3 * bi + 2)
                        nc.vector.scalar_tensor_tensor(out=soft[:, bi], in0=soft_ln, scalar=0.0,
                                                       in1=soft[:, bi], op0=ALU.min, op1=ALU.add).then_inc(soft_made, 1)
                if n == 27 and front:
                    if slot == 0:
                        dve.wait_ge(soft_made, 6 * w + 3)
                        nc.vector.tensor_tensor(dt[par][:, :, 0, :], dt[par][:, :, 0, :], soft[:, 0],
                                                ALU.add).then_inc(dt_dve, 1)
                    elif slot == 1:
                        dve.wait_ge(dt_dve, 2 * w + 1)
                        dve.wait_ge(silu_made, 2 * w + 1)
                        nc.vector.tensor_tensor(dtu[par][:, :, 0, :], dt[par][:, :, 0, :],
                                                xc[par][:, :, 0, :], ALU.mult).then_inc(dt_dve, 1)
                if q in (9, 10) and back:
                    take_y(w - 2, 1, par, ("outproj0", w - 1), q - 9)
                if q == 12 and back:
                    gate_y(w - 2, 1, par)
                if q == 19 and back:
                    take_v("outproj1", w, 1)
                if 20 <= q < 25 and back:
                    if q == 20:
                        dve.wait_ge(drained[bank_of("outproj1")], count_of("outproj1", w))
                    statistics(v, st_attn, attn_stat, 4 * (w - 2), q - 20)
                if q == 33 and back:
                    dve.wait_ge(x1_scaled, 2 * (w - 1))
                    dve.wait_ge(xb_in, 16 * (w - 1))
                    nc.vector.tensor_tensor(x1[:], x1[:], xb[:], ALU.add).then_inc(x1_made, 1)
                if q == 30 and back:
                    dve.wait_ge(attn_rstd, 2 * (w - 1))
                    shift_of(st_attn, st_attn["rstd"][:], attn_shift)
                if q in (31, 32) and back:
                    dve.wait_ge(attn_shift, w - 1)
                    dve.wait_ge(out_made, w - 1)
                    normalize(x1, v, st_attn["rstd"], st_attn, q - 31, x1_scaled)
                if 34 <= q < 39 and back:
                    if q == 34:
                        dve.wait_ge(x1_made, w - 1)
                    statistics(x1, st_mid, mid_stat, 4 * (w - 2), q - 34)
                if q == 42 and back:
                    dve.wait_ge(mid_rstd, 2 * (w - 1))
                    shift_of(st_mid, st_mid["rstd"][:], mid_shift)
                if q in (43, 44) and back:
                    dve.wait_ge(mid_shift, w - 1)
                    normalize(f, x1, st_mid["rstd"], st_mid, q - 43, f_made)
                if q in (80, 83) and back:
                    bi = (q - 80) // 3
                    b = bank_of(f"value{bi}")
                    tiles = slice(bi * TILES, (bi + 1) * TILES)
                    dve.wait_ge(filled[b], count_of(f"value{bi}", w))
                    nc.vector.scalar_tensor_tensor(out=o[:, tiles, :], in0=gate[:, tiles, :], scalar=1.0,
                                                   in1=misc[b][:].rearrange("p (j d) -> p j d", d=P),
                                                   op0=ALU.add, op1=ALU.mult).then_inc(drained[b], 1)
                if 86 <= q < 91 and back:
                    if q < 88:
                        g = f"value{q - 86}"
                        dve.wait_ge(drained[bank_of(g)], count_of(g, w))
                    statistics(o, st_out, out_stat, 4 * (w - 2), q - 86)
                if q == 93 and back:
                    dve.wait_ge(out_rstd, 2 * (w - 1))
                    shift_of(st_out, st_out["rstd"][:], out_shift)
                if q in (94, 95) and back:
                    dve.wait_ge(out_shift, w - 1)
                    normalize(o, o, st_out["rstd"], st_out, q - 94, o_scaled)
                if q in (57, 58) and scan:
                    take_y(w - 1, 0, 1 - par, ("outproj1", w), q - 57)
                if q == 60 and scan:
                    gate_y(w - 1, 0, 1 - par)
                if q == 62 and scan:
                    nc.vector.tensor_copy(r1_back[:], front_rstds[1 - par][:, 0]).then_inc(r1_kept, 1)
                if q == 69 and scan:
                    dve.wait_ge(r1_kept, w)
                    dve.wait_ge(xb_in, 16 * w)
                    take_v("outproj0", w, 0)

            def body(w, par, front, scan, back):
                for n in range(STEPS):
                    if scan and n + DBU_AHEAD < STEPS:
                        make_dbu(w - 1, 1 - par, n + DBU_AHEAD)
                    elif scan and front:
                        make_dbu(w, par, n + DBU_AHEAD - STEPS)
                    side_work(w, par, front, scan, back, n, 0)
                    for half in range(HALVES):
                        if scan:
                            t = (w - 1) * STEPS + n
                            if half == 0:
                                wait(dve, prod_made, t + 1 - RING)
                                if by_pool(n):
                                    dve.wait_ge(dbu_pool, pool_made(w - 1, n) + 1)
                                else:
                                    dve.wait_ge(dbu_dve, dve_made(w - 1, n) + 1)
                            dve.wait_ge(da_made, 2 * t + half + 1)
                            nc.vector.tensor_tensor_scan(h[:, n % RING, half], da[half][:], dbu[:, n % RING, half], 0.0,
                                                         ALU.mult, ALU.add).then_inc(scanned, 1)
                        side_work(w, par, front, scan, back, n, half + 1)
                if front and not scan:
                    for n in range(DBU_AHEAD):
                        make_dbu(w, par, n)

            bodies(dve, body)

        @block.tensor
        def _(pe):
            pe.wait_ge(ident_made, 2)
            pe.wait_ge(weights_in, 19 * 16)
            pe.wait_ge(scaled_w, HALVES * TAPS + 1)
            tr = lambda dst, src: nc.tensor.transpose(dst, src, ident[:])
            for half in range(HALVES):
                cols = slice(half * P, (half + 1) * P)
                for k in range(TAPS):
                    tr(bank[half][:, k * P:(k + 1) * P], tap_w[:, half, k])
                tr(bank[2][:, cols], in_w[:, 2 + half, :])
                tr(bank[2][:, 2 * P + half * P:2 * P + (half + 1) * P], xp_rows[:, cols])
                tr(bank[3][:, cols], out_w[:, cols])
                tr(bank[3][0:RANK, 2 * P + half * P:2 * P + (half + 1) * P], dt_w_rows[:, half, :])
            for i in range(3):
                last = tr(bank[4][:, i * P:(i + 1) * P], mix_w[:, i, :])
            last.then_inc(w_transposed, 1)
            pe.wait_ge(w_drained, 1)
            pe.wait_ge(mix_made, 3)
            pe.wait_ge(spread_made, 4)
            pe.wait_ge(consts_made, 1)

            def bank_free(group, w):
                b = bank_of(group)
                wait(pe, drained[b], count_of(group, w) - 1)
                return misc[b]

            def done(group, last):
                last.then_inc(filled[bank_of(group)], 1)

            def skip(groups, w):
                for g in groups:
                    bank_free(g, w)
                    pe.sem_inc(filled[bank_of(g)], 1)
                    pe.sem_inc(drained[bank_of(g)], 1)

            def evacuated(group, w):
                pe.wait_ge(drained[bank_of(group)], count_of(group, w))

            def spread_b(pair, par, n):
                bi, s = n // S, n % S
                if s == 0:
                    pe.wait_ge(parts_made, 4 * pair + 2 * bi + 2)
                before = pair * STEPS + n - 1
                if not isinstance(before, int) or before >= 0:
                    if by_pool(n - 1):
                        pe.wait_ge(b_copied, pool_made(pair, n))
                    else:
                        pe.wait_ge(dbu_dve, dve_made(pair, n))
                nc.tensor.matmul(b_ps[:], spread[:, s, :], parts[par][:, bi, :],
                                 start=True, stop=True).then_inc(b_spread, 1)

            def spread_c(pair, par, n):
                bi, s = n // S, n % S
                wait(pe, c_copied, pair * STEPS + n)
                nc.tensor.matmul(c_ps[:], spread[:, S + s, :], parts[par][:, bi, :],
                                 start=True, stop=True).then_inc(c_spread, 1)

            def add_states(w, n):
                t = (w - 1) * STEPS + n
                s = n % S
                if s == 0:
                    wait(pe, y_taken, 2 * (w - 1) + n // S)
                pe.wait_ge(prod_made, t + 1)
                for half in range(HALVES):
                    last = nc.tensor.matmul(y_acc[half][:], ident[:], prod[:, n % RING, half],
                                            start=(s == 0), stop=(s == S - 1))
                last.then_inc(y_added, 1)

            def transposes(group, w, src, bi):
                dst = bank_free(group, w)
                for j in range(TILES):
                    last = nc.tensor.transpose(dst[:, j * P:(j + 1) * P], src[:, bi * TILES + j, :], ident[:])
                done(group, last)

            def out_project(group, w, part):
                dst = bank_free(group, w) if part == 0 else misc[bank_of(group)]
                for j in range(2 * part, 2 * part + 2):
                    for half in range(HALVES):
                        last = nc.tensor.matmul(dst[:, j * P:(j + 1) * P], yg[:, half, j * P:(j + 1) * P],
                                                out_wT[:, half, :], start=(half == 0), stop=(half == HALVES - 1))
                if part == 1:
                    done(group, last)

            def mix_key(bi, w):
                g = f"key{bi}"
                evacuated(f"back_tr{bi}", w)
                dst = bank_free(g, w)
                nc.tensor.matmul(dst[:], mix_now[:, 1], fT[:, bi, 1:L + 1], start=True, stop=False)
                done(g, nc.tensor.matmul(dst[:], mix_before[:, 1], fT[:, bi, 0:L], start=False, stop=True))

            def mix_gate(bi, w):
                g = f"gate{bi}"
                dst = bank_free(g, w)
                for j in range(TILES):
                    nc.tensor.matmul(dst[:, j * P:(j + 1) * P], fT[:, bi, j * P + 1:(j + 1) * P + 1],
                                     mix_now[:, 0], start=True, stop=False)
                    last = nc.tensor.matmul(dst[:, j * P:(j + 1) * P], fT[:, bi, j * P:(j + 1) * P],
                                            mix_before[:, 0], start=False, stop=True)
                done(g, last)

            def side_work(w, par, front, scan, back, n, slot):
                if n == 5:
                    if back:
                        pe.wait_ge(y_gated, 2 * (w - 1))
                        out_project("outproj1", w, slot)
                    elif slot == 0:
                        skip(["outproj1"], w)
                if n == 4:
                    if front:
                        pe.wait_ge(hn_made, 2 * w + slot + 1)
                        transposes(f"front_tr{slot}", w, hn, slot)
                    else:
                        skip([f"front_tr{slot}"], w)
                if 6 <= n < 14 and front:
                    k = 2 * (n - 6) + slot
                    bi, half, back_by = k // (2 * TAPS), k // TAPS % 2, k % TAPS
                    g = f"conv{bi}{half}"
                    if back_by == 0:
                        evacuated(f"front_tr{bi}", w)
                        bank_free(g, w)
                    last = nc.tensor.matmul(misc[bank_of(g)][:, back_by:L], tap_wT[:, half, TAPS - 1 - back_by],
                                            hT[:, bi, 0:L - back_by], start=(back_by == 0),
                                            stop=(back_by == TAPS - 1))
                    if back_by == TAPS - 1:
                        done(g, last)
                if n in (14, 15) and front:
                    bi = n - 14
                    g = f"z{bi}{slot}"
                    done(g, nc.tensor.matmul(bank_free(g, w)[:], z_wT[:, slot], hT[:, bi, :], start=True, stop=True))
                if (n, slot) == (15, 1) and not front:
                    skip([f"{a}{bi}{half}" for a in ("conv", "z") for bi in range(2) for half in range(2)], w)
                if n == 16:
                    if back:
                        pe.wait_ge(f_made, 2 * (w - 2) + slot + 1)
                        transposes(f"back_tr{slot}", w, f, slot)
                    else:
                        skip([f"back_tr{slot}"], w)
                if back:
                    if (n, slot) == (17, 1):
                        mix_key(0, w)
                    if (n, slot) == (18, 0):
                        mix_key(1, w)
                    if (n, slot) == (18, 1):
                        mix_gate(0, w)
                    if (n, slot) == (19, 0):
                        mix_gate(1, w)
                elif (n, slot) == (19, 0):
                    skip(["key0", "key1", "gate0", "gate1"], w)
                if n == 21:
                    if scan:
                        pe.wait_ge(y_gated, 2 * (w - 1) + 1)
                        out_project("outproj0", w, slot)
                    elif slot == 0:
                        skip(["outproj0"], w)
                if n in (20, 22):
                    bi, half = (n - 20) // 2, slot
                    g = f"xproj{bi}"
                    if front:
                        if half == 0:
                            pe.wait_ge(silu_made, 2 * w + 1)
                            bank_free(g, w)
                        last = nc.tensor.matmul(misc[bank_of(g)][:], xp_wT[:, half], xc[par][:, half, bi, :],
                                                start=(half == 0), stop=(half == HALVES - 1))
                        if half == 1:
                            done(g, last)
                    elif half == 0:
                        skip([g], w)
                if n in (23, 27):
                    bi, half = (n - 23) // 4, slot
                    g = f"dt{bi}{half}"
                    if front:
                        pe.wait_ge(hi_made, 2 * w + bi + 1)
                        done(g, nc.tensor.matmul(bank_free(g, w)[:], dt_wT[:, half], dt_low[:, bi, :],
                                                 start=True, stop=True))
                    else:
                        skip([g], w)
                if n == 25:
                    g = f"value{slot}"
                    if back:
                        pe.wait_ge(key_squared, w - 1)
                        dst = bank_free(g, w)
                        for j in range(TILES):
                            last = nc.tensor.matmul(dst[:, j * P:(j + 1) * P], key[:, slot, j * P:(j + 1) * P],
                                                    mix_wT[:, 2], start=True, stop=True)
                        done(g, last)
                    else:
                        skip([g], w)

            def body(w, par, front, scan, back):
                for n in range(STEPS):
                    if scan:
                        if n + B_AHEAD < STEPS:
                            spread_b(w - 1, 1 - par, n + B_AHEAD)
                        elif front:
                            spread_b(w, par, n + B_AHEAD - STEPS)
                        if n + 1 < STEPS:
                            spread_c(w - 1, 1 - par, n + 1)
                        elif front:
                            spread_c(w, par, 0)
                    side_work(w, par, front, scan, back, n, 0)
                    if scan and n >= LAG:
                        add_states(w, n - LAG)
                    if n < LAG and back:
                        add_states(w - 1, n - LAG + STEPS)
                    side_work(w, par, front, scan, back, n, 1)
                if front and not scan:
                    spread_c(w, par, 0)
                    for n in range(B_AHEAD):
                        spread_b(w, par, n)

            bodies(pe, body)


_INS = ["L0_attn_x", "L0_attn_ln_gamma", "L0_attn_ln_beta", "L0_attn_in_proj_w", "L0_attn_conv_w",
        "L0_attn_conv_b", "L0_attn_x_proj_w", "L0_attn_dt_proj_w", "L0_attn_dt_proj_b", "L0_attn_A_log",
        "L0_attn_D", "L0_attn_out_proj_w", "L0_ffn_W_r", "L0_ffn_W_k", "L0_ffn_W_v", "L0_ffn_mu_r",
        "L0_ffn_mu_k"]


def kernel(**inputs):
    import numpy as np
    import concourse.bacc as bacc
    from concourse import mybir as _mybir
    from concourse.bass_utils import run_bass_kernel_spmd

    nc = bacc.Bacc("TRN2", target_bir_lowering=False, num_devices=1)
    arrays, args = {}, []
    for name in _INS:
        a = np.ascontiguousarray(inputs[name])
        arrays[f"in_{name}"] = a
        args.append(nc.dram_tensor(f"in_{name}", a.shape, _mybir.dt.from_np(a.dtype), kind="ExternalInput").ap())
    shape = inputs["L0_attn_x"].shape
    args.append(nc.dram_tensor("out", shape, _mybir.dt.float32, kind="ExternalOutput").ap())
    mamba_sandwich(nc, *args)
    r = run_bass_kernel_spmd(nc, [arrays], core_ids=[0])
    return r.results[0]["out"]
```

```python
from contextlib import ExitStack

import concourse.bass as bass
from concourse import mybir

FP32 = mybir.dt.float32
BF16 = mybir.dt.bfloat16
ALU = mybir.AluOpType
ACT = mybir.ActivationFunctionType

EPS = 1e-5
EXP_LN_SET = "natural_log_exp_and_others"
SILU_TANH_SET = "silu_and_others"
P = 128
L = 512
S = 16
HALVES = 2
TAPS = 4
RANK = 8
TILES = L // P
PT = 2 * TILES
STEPS = 2 * S
LAG = 3
B_AHEAD = 3
DBU_AHEAD = 2
POOL_AHEAD = 4
RING = 4
POOL_STEPS = (2, 3, 6, 9, 14, 17, 23, 29, 30)

GROUPS = ["front_tr0", "front_tr1", "conv00", "outproj1", "conv01", "conv10", "conv11",
          "z00", "z01", "z10", "z11", "back_tr0", "back_tr1", "key0", "key1", "gate0", "gate1",
          "outproj0", "xproj0", "xproj1", "dt00", "dt01", "value0", "value1", "dt10", "dt11"]
PER_BANK = len(GROUPS) // 2


def bank_of(group):
    return GROUPS.index(group) % 2


def count_of(group, w):
    return w * PER_BANK + (GROUPS.index(group) // 2 + 1)


def by_pool(n):
    return n % STEPS in POOL_STEPS


def pool_made(pair, n):
    return pair * len(POOL_STEPS) + sum(by_pool(i) for i in range(n))


def dve_made(pair, n):
    return pair * (STEPS - len(POOL_STEPS)) + sum(not by_pool(i) for i in range(n))


def wait(engine, semaphore, value):
    if not isinstance(value, int) or value > 0:
        engine.wait_ge(semaphore, value)


def mamba_sandwich(nc, x, ln_gamma, ln_beta, in_proj_w, conv_w, conv_b, x_proj_w, dt_proj_w,
                   dt_proj_b, A_log, D, out_proj_w, W_r, W_k, W_v, mu_r, mu_k, out):
    pairs = x.shape[0] // 2
    x_pairs = x.rearrange("(w b) (j p) d -> w p (b j) d", b=2, p=P)
    out_pairs = out.rearrange("(w b) (j p) d -> w p (b j) d", b=2, p=P)

    ctx = ExitStack()
    with ctx:
        def sb(name, shape, dt=FP32):
            return ctx.enter_context(nc.sbuf_tensor(name, shape, dt))

        def sem(name):
            return ctx.enter_context(nc.semaphore(name))

        h = sb("h", [P, RING, HALVES, L])
        staged = h[:].rearrange("p a b (c d) -> p (a b c) d", d=P)
        in_w = staged[:, 0:4]
        conv_taps = sb("conv_taps", [P, HALVES, TAPS])
        conv_bias = sb("conv_bias", [P, HALVES])
        xp_rows = staged[:, 4:6].rearrange("p a d -> p (a d)")
        dt_w_rows = sb("dt_w_rows", [P, HALVES, RANK])
        dt_bias = sb("dt_bias", [P, HALVES])
        a_log = sb("a_log", [P, HALVES, S])
        d_skip = sb("d_skip", [P, HALVES])
        out_w = staged[:, 6:8].rearrange("p a d -> p (a d)")
        mix_w = staged[:, 8:11]
        mix_mu = sb("mix_mu", [P, 2])
        gamma_beta = sb("gamma_beta", [P, 2])

        ident = sb("ident", [P, P])
        ident_bf = sb("ident_bf", [P, P], BF16)
        pick = sb("pick", [P, 2 * S], BF16)
        spread = sb("spread", [P, 2 * S, P], BF16)
        eps_col = sb("eps_col", [P, 1])
        eps_sq_col = sb("eps_sq_col", [P, 1])
        one_col = sb("one_col", [P, 1])
        tap_wT = sb("tap_wT", [P, HALVES, TAPS, P])
        z_wT = sb("z_wT", [P, HALVES, P])
        xp_wT = sb("xp_wT", [P, HALVES, P])
        dt_wT = sb("dt_wT", [RANK, HALVES, P])
        neg_a = sb("neg_a", [P, HALVES, S])
        out_wT = sb("out_wT", [P, HALVES, P])
        mix_wT = sb("mix_wT", [P, 3, P])
        one_minus_mu = sb("one_minus_mu", [P, 2])
        mix_now = sb("mix_now", [P, 2, P])
        mix_before = sb("mix_before", [P, 2, P])

        xf = sb("xf", [P, PT, P])
        hn = sb("hn", [P, PT, P])
        tap_w = hn[:].rearrange("p (h k) d -> p h k d", h=HALVES)
        hT = sb("hT", [P, 2, L])
        xc = [sb(f"xc{i}", [P, HALVES, 2, L]) for i in range(2)]
        zs = [sb(f"zs{i}", [P, HALVES, 2, L]) for i in range(2)]
        dt = [sb(f"dt{i}", [P, HALVES, 2, L]) for i in range(2)]
        dtu = [sb(f"dtu{i}", [P, HALVES, 2, L]) for i in range(2)]
        parts = [sb(f"parts{i}", [P, 2, L], BF16) for i in range(2)]
        low_rest = sb("low_rest", [P, 2, L])
        dt_low = low_rest[0:RANK]
        rest = low_rest[:, 0]
        soft = sb("soft", [P, 2, HALVES, L])
        soft_lin = hn[:].rearrange("p (a t) d -> p a (t d)", a=HALVES)

        dbu = sb("dbu", [P, RING, HALVES, L])
        b_sb = sb("b_sb", [P, 2, L])
        c_sb = sb("c_sb", [P, RING, L])
        prod = sb("prod", [P, RING, HALVES, L])

        xb = sb("xb", [P, PT, P])
        yg = sb("yg", [P, HALVES, L])
        soft_ln = yg
        v = sb("v", [P, PT, P])
        x1 = sb("x1", [P, PT, P])
        f = v
        fT = sb("fT", [P, 2, L + 1])
        key = sb("key", [P, 2, L])
        o = sb("o", [P, PT, P])
        gate = o

        def stat_tiles(name):
            return {k: sb(f"{name}_{k}", [P, PT] + ([6] if k == "bn" else []))
                    for k in ("bn", "sum2", "dif", "m2", "sq", "var", "shift")
                             + (() if name == "front" else ("ln", "rstd"))}

        st_front, st_attn, st_mid, st_out = (stat_tiles(n) for n in ("front", "attn", "mid", "out"))
        front_lns = sb("front_lns", [P, 2, PT])
        front_rstds = [sb(f"front_rstds{i}", [P, 2, PT]) for i in range(2)]
        r1_back = sb("r1_back", [P, PT])

        bank = [ctx.enter_context(nc.psum_tensor(f"bank{i}", [P, L], FP32)) for i in range(8)]
        misc, da, y_acc, b_ps, c_ps = bank[0:2], bank[2:4], bank[4:6], bank[6], bank[7]

        weights_in, weights_cleared = sem("weights_in"), sem("weights_cleared")
        ident_made, consts_made, scaled_w = sem("ident_made"), sem("consts_made"), sem("scaled_w")
        w_transposed, w_drained, a_made = sem("w_transposed"), sem("w_drained"), sem("a_made")
        spread_made, mix_made = sem("spread_made"), sem("mix_made")
        filled = [sem("misc_filled0"), sem("misc_filled1")]
        drained = [sem("misc_drained0"), sem("misc_drained1")]
        xf_in, xb_in, out_stored = sem("xf_in"), sem("xb_in"), sem("out_stored")
        front_stat, front_rstd, hn_made = sem("front_stat"), sem("front_rstd"), sem("hn_made")
        silu_made, key_squared, soft_exp, ln_made = sem("silu_made"), sem("key_squared"), sem("soft_exp"), sem("ln_made")
        hi_made, parts_made, soft_made = sem("hi_made"), sem("parts_made"), sem("soft_made")
        dt_dve, dt_pool = sem("dt_dve"), sem("dt_pool")
        b_spread, b_copied, c_spread, c_copied = sem("b_spread"), sem("b_copied"), sem("c_spread"), sem("c_copied")
        da_made, dbu_dve, dbu_pool, scanned = sem("da_made"), sem("dbu_dve"), sem("dbu_pool"), sem("scanned")
        prod_made, y_added = sem("prod_made"), sem("y_added")
        y_taken, y_gated, r1_kept, v_made = sem("y_taken"), sem("y_gated"), sem("r1_kept"), sem("v_made")
        attn_stat, attn_rstd, x1_scaled, x1_made = sem("attn_stat"), sem("attn_rstd"), sem("x1_scaled"), sem("x1_made")
        mid_stat, mid_rstd, f_made = sem("mid_stat"), sem("mid_rstd"), sem("f_made")
        out_stat, out_rstd, o_scaled, out_made = sem("out_stat"), sem("out_rstd"), sem("o_scaled"), sem("out_made")
        front_shift, attn_shift, mid_shift, out_shift = (sem(f"{n}_shift") for n in ("front", "attn", "mid", "out"))

        def bodies(engine, body):
            body(0, 0, front=True, scan=False, back=False)
            body(1, 1, front=True, scan=True, back=False)
            with engine.Fori(2, pairs, 2) as w:
                body(w, 0, front=True, scan=True, back=True)
                body(w + 1, 1, front=True, scan=True, back=True)
            body(pairs, 0, front=False, scan=True, back=True)
            body(pairs + 1, 1, front=False, scan=False, back=True)

        block = ctx.enter_context(nc.Block())

        @block.sync
        def _(sp):
            def load_column(dst, vector):
                sp.dma_start(dst, vector.rearrange("(h p) -> p h", p=P),
                             allow_slow_non_contiguous=True).then_inc(weights_in, 16)

            sp.dma_start(xf[:], x_pairs[0]).then_inc(xf_in, 16)
            sp.sem_inc(out_stored, 16)
            sp.dma_start(in_w, in_proj_w.rearrange("(c p) d -> p c d", p=P)).then_inc(weights_in, 16)
            sp.dma_start(conv_taps[:], conv_w.rearrange("(h p) k -> p h k", p=P)).then_inc(weights_in, 16)
            load_column(conv_bias[:], conv_b)
            sp.dma_start(dt_w_rows[:], dt_proj_w.rearrange("(h p) r -> p h r", p=P)).then_inc(weights_in, 16)
            load_column(dt_bias[:], dt_proj_b)
            sp.dma_start(a_log[:], A_log.rearrange("(h p) s -> p h s", p=P)).then_inc(weights_in, 16)
            load_column(d_skip[:], D)
            sp.dma_start(out_w, out_proj_w).then_inc(weights_in, 16)
            for i, wt in enumerate((W_r, W_k, W_v)):
                sp.dma_start(mix_w[:, i, :], wt).then_inc(weights_in, 16)
            for i, mu in enumerate((mu_r, mu_k)):
                load_column(mix_mu[:, i:i + 1], mu)
            for i, g in enumerate((ln_gamma, ln_beta)):
                load_column(gamma_beta[:, i:i + 1], g)
            sp.wait_ge(weights_cleared, 1)
            sp.dma_start(xp_rows[0:RANK, :], x_proj_w[0:RANK, :]).then_inc(weights_in, 16)
            for i in range(1, 4):
                sp.dma_start(xp_rows[32 * i:32 * i + 2 * S, :],
                             x_proj_w[RANK:RANK + 2 * S, :]).then_inc(weights_in, 16)

            def body(w, par, front, scan, back):
                if front:
                    sp.wait_ge(hn_made, 2 * w + 2)
                    following = pairs - 1 if isinstance(w, int) and w == pairs - 1 else w + 1
                    sp.dma_start(xf[:], x_pairs[following]).then_inc(xf_in, 16)
                if scan:
                    wait(sp, x1_made, w - 1)
                    sp.dma_start(xb[:], x_pairs[w - 1]).then_inc(xb_in, 16)
                if back:
                    sp.wait_ge(out_made, w)
                    sp.dma_start(out_pairs[w - 2], o[:]).then_inc(out_stored, 16)

            body(0, 0, True, False, False)
            body(1, 1, True, True, False)
            with sp.Fori(2, pairs - 2, 2) as w:
                body(w, 0, True, True, True)
                body(w + 1, 1, True, True, True)
            body(pairs - 2, 0, True, True, True)
            body(pairs - 1, 1, True, True, True)
            body(pairs, 0, False, True, True)
            body(pairs + 1, 1, False, False, True)
            sp.wait_ge(out_stored, 16 * (pairs + 1))

        @block.gpsimd
        def _(pool):
            nc.gpsimd.memset(ident[:], 0.0).then_inc(ident_made, 1)
            pool.wait_ge(ident_made, 1)
            nc.gpsimd.affine_select(out=ident[:], in_=ident[:], compare_op=ALU.not_equal, fill=1.0,
                                    base=0, pattern=[[-1, P]], channel_multiplier=1).then_inc(ident_made, 1)
            pool.sem_inc(out_made, 1)

            def make_dbu(pair, par, n):
                if not by_pool(n):
                    return
                bi = n // S
                pool.wait_ge(b_copied, pool_made(pair, n) + 1)
                pool.wait_ge((dt_dve, dt_pool)[bi], 2 * pair + 2)
                wait(pool, scanned, 2 * (pair * STEPS + n + 1 - RING))
                nc.gpsimd.tensor_tensor(dbu[:, n % RING], dtu[par][:, :, bi, :],
                                        b_sb[:, sum(by_pool(i) for i in range(n)) % 2].unsqueeze(1).to_broadcast([P, HALVES, L]),
                                        ALU.mult).then_inc(dbu_pool, 1)

            def body(w, par, front, scan, back):
                for n in range(STEPS):
                    if scan:
                        t = (w - 1) * STEPS + n
                        pool.wait_ge(scanned, 2 * t + 2)
                        pool.wait_ge(c_copied, t + 1)
                        wait(pool, y_added, t + 1 - RING)
                        nc.gpsimd.tensor_tensor(
                            prod[:, n % RING], h[:, n % RING],
                            c_sb[:, n % RING].unsqueeze(1).to_broadcast([P, HALVES, L]),
                            ALU.mult).then_inc(prod_made, 1)
                        if n + POOL_AHEAD < STEPS:
                            make_dbu(w - 1, 1 - par, n + POOL_AHEAD)
                        elif front:
                            make_dbu(w, par, n + POOL_AHEAD - STEPS)
                    if n == 8 and scan:
                        pool.wait_ge(soft_made, 6 * w)
                        nc.gpsimd.tensor_tensor(dt[1 - par][:, :, 1, :], dt[1 - par][:, :, 1, :], soft[:, 1],
                                                ALU.add).then_inc(dt_pool, 1)
                    if n == 9 and scan:
                        pool.wait_ge(dt_pool, 2 * w - 1)
                        nc.gpsimd.tensor_tensor(dtu[1 - par][:, :, 1, :], dt[1 - par][:, :, 1, :],
                                                xc[1 - par][:, :, 1, :], ALU.mult).then_inc(dt_pool, 1)
                    if n == 31 and back:
                        pool.wait_ge(o_scaled, 2 * (w - 1))
                        nc.gpsimd.tensor_tensor(o[:], o[:], x1[:], ALU.add).then_inc(out_made, 1)
                if front and not scan:
                    for n in range(POOL_AHEAD):
                        make_dbu(w, par, n)

            bodies(pool, body)

        @block.scalar
        def _(act):
            nc.scalar.preload_act_table_set(EXP_LN_SET)
            act.wait_ge(consts_made, 1)

            def front_rstd_of(e, parity, step):
                if step == 0:
                    act.wait_ge(front_stat, 4 * e + 4)
                    nc.scalar.activation(front_lns[:, 0], st_front["var"][:], ACT.Ln, bias=eps_col[:], scale=1.0 / P)
                    nc.scalar.activation(front_lns[:, 1], st_front["var"][:], ACT.Ln, bias=eps_sq_col[:],
                                         scale=(1.0 + EPS) / P).then_inc(front_rstd, 1)
                else:
                    act.wait_ge(front_rstd, 2 * e + 1)
                    wait(act, r1_kept, e - 1)
                    nc.scalar.activation(front_rstds[parity][:], front_lns[:], ACT.Exp, scale=-0.5).then_inc(front_rstd, 1)

            for step in range(2):
                front_rstd_of(0, 0, step)
            act.wait_ge(weights_in, 19 * 16)
            nc.scalar.activation(neg_a[:], a_log[:], ACT.Exp).then_inc(a_made, 1)

            def rstd(out_, ln_, var_, semaphore, base, step):
                if step == 0:
                    nc.scalar.activation(ln_[:], var_[:], ACT.Ln, bias=eps_col[:], scale=1.0 / P).then_inc(semaphore, 1)
                else:
                    act.wait_ge(semaphore, base + 1)
                    nc.scalar.activation(out_[:], ln_[:], ACT.Exp, scale=-0.5).then_inc(semaphore, 1)

            def evacuate(group, w, out_, func, **kw):
                b = bank_of(group)
                act.wait_ge(filled[b], count_of(group, w))
                nc.scalar.activation(out_, misc[b][:], func, **kw).then_inc(drained[b], 1)

            def copy_b(pair, n):
                if not by_pool(n):
                    return
                act.wait_ge(b_spread, pair * STEPS + n + 1)
                wait(act, dbu_pool, pool_made(pair, n) - 1)
                nc.scalar.activation(b_sb[:, sum(by_pool(i) for i in range(n)) % 2], b_ps[:], ACT.Copy).then_inc(b_copied, 1)

            def log_of_softplus(e, bi):
                act.wait_ge(soft_exp, 2 * e + bi + 1)
                wait(act, soft_made, 6 * e + 3 * bi)
                nc.scalar.activation(soft_ln[:], soft[:, bi], ACT.Ln, bias=one_col[:]).then_inc(ln_made, 1)

            def side_work(w, par, front, scan, back, n, slot):
                if n == 31 and front:
                    front_rstd_of(w + 1, 1 - par, slot)
                if n == 2 and front:
                    evacuate(f"front_tr{slot}", w, hT[:, slot, :], ACT.Identity,
                             bias=gamma_beta[:, 1:2], scale=gamma_beta[:, 0:1])
                if n == 9 and back:
                    if slot == 0:
                        act.wait_ge(attn_stat, 4 * (w - 1))
                    rstd(st_attn["rstd"], st_attn["ln"], st_attn["var"], attn_rstd, 2 * (w - 2), slot)
                if n in (5, 8, 10, 12) and slot == 1 and front:
                    bi, half = (n - 6) // 4 if n > 5 else 0, (n - 6) // 2 % 2 if n > 5 else 0
                    if n == 5:
                        wait(act, y_taken, 2 * (w - 1))
                    evacuate(f"conv{bi}{half}", w, xc[par][:, half, bi, :], ACT.Identity,
                             bias=conv_bias[:, half:half + 1])
                if n == 14 and back:
                    if slot == 0:
                        act.wait_ge(mid_stat, 4 * (w - 1))
                    rstd(st_mid["rstd"], st_mid["ln"], st_mid["var"], mid_rstd, 2 * (w - 2), slot)
                if 13 <= n < 17 and slot == 1 and front:
                    bi, half = (n - 13) // 2, (n - 13) % 2
                    if n == 13:
                        wait(act, y_gated, 2 * (w - 1))
                    evacuate(f"z{bi}{half}", w, zs[par][:, half, bi, :], ACT.Identity)
                if (n, slot) in ((16, 1), (17, 0)) and back:
                    bi = 1 - slot
                    evacuate(f"back_tr{bi}", w, fT[:, bi, 1:L + 1], ACT.Identity)
                if (n, slot) in ((18, 0), (18, 1)) and back:
                    bi = ((18, 0), (18, 1)).index((n, slot))
                    evacuate(f"key{bi}", w, key[:, bi, :], ACT.Relu)
                if (n, slot) == (20, 1) and back:
                    for bi in range(2):
                        act.wait_ge(drained[bank_of(f"key{bi}")], count_of(f"key{bi}", w))
                    nc.scalar.activation(key[:], key[:], ACT.Square).then_inc(key_squared, 1)
                if (n, slot) == (19, 1):
                    nc.scalar.preload_act_table_set(SILU_TANH_SET)
                    if front:
                        for g in ("z10", "z11"):
                            act.wait_ge(drained[bank_of(g)], count_of(g, w))
                        nc.scalar.activation(xc[par][:], xc[par][:], ACT.Silu).then_inc(silu_made, 1)
                    if back:
                        act.wait_ge(out_stored, 16 * (w - 1))
                        for bi in range(2):
                            evacuate(f"gate{bi}", w, gate[:, bi * TILES:(bi + 1) * TILES, :], ACT.Tanh, scale=0.5)
                    if front:
                        nc.scalar.activation(zs[par][:], zs[par][:], ACT.Silu).then_inc(silu_made, 1)
                    nc.scalar.preload_act_table_set(EXP_LN_SET)
                if n in (22, 23) and slot == 1 and front:
                    bi = n - 22
                    b = bank_of(f"xproj{bi}")
                    act.wait_ge(filled[b], count_of(f"xproj{bi}", w))
                    nc.scalar.activation(dt_low[:, bi, :], misc[b][0:RANK, :], ACT.Copy)
                    nc.scalar.activation(parts[par][:, bi, :], misc[b][:], ACT.Copy).then_inc(hi_made, 1)
                if n in (24, 28) and front:
                    bi, half = (n - 24) // 4, slot
                    b = bank_of(f"dt{bi}{half}")
                    act.wait_ge(filled[b], count_of(f"dt{bi}{half}", w))
                    nc.scalar.activation(soft[:, bi, half], misc[b][:], ACT.Abs, bias=dt_bias[:, half:half + 1])
                    nc.scalar.activation(dt[par][:, half, bi, :], misc[b][:], ACT.Relu,
                                         bias=dt_bias[:, half:half + 1]).then_inc(drained[b], 1)
                if (n, slot) in ((25, 0), (30, 0)) and front:
                    bi = (n - 25) // 4
                    for half in range(HALVES):
                        act.wait_ge(drained[bank_of(f"dt{bi}{half}")], count_of(f"dt{bi}{half}", w))
                    nc.scalar.activation(soft[:, bi], soft[:, bi], ACT.Exp, scale=-1.0).then_inc(soft_exp, 1)
                if (n, slot) == (25, 1) and front:
                    log_of_softplus(w, 0)
                if (n, slot) == (7, 1) and scan:
                    b = bank_of("outproj1")
                    act.wait_ge(filled[b], count_of("outproj1", w))
                    log_of_softplus(w - 1, 1)
                if n == 30 and back:
                    if slot == 0:
                        act.wait_ge(out_stat, 4 * (w - 1))
                    rstd(st_out["rstd"], st_out["ln"], st_out["var"], out_rstd, 2 * (w - 2), slot)

            def body(w, par, front, scan, back):
                for n in range(STEPS):
                    for half in range(HALVES):
                        if scan:
                            t = (w - 1) * STEPS + n
                            bi, s = n // S, n % S
                            if s == 0 and half == 0:
                                act.wait_ge((dt_dve, dt_pool)[bi], 2 * w - 1)
                            wait(act, scanned, 2 * t - 1 + half)
                            nc.scalar.activation(da[half][:], dt[1 - par][:, half, bi, :], ACT.Exp,
                                                 scale=neg_a[:, half, s:s + 1]).then_inc(da_made, 1)
                            if half == 0:
                                act.wait_ge(c_spread, t + 1)
                                wait(act, prod_made, t + 1 - RING)
                                nc.scalar.activation(c_sb[:, n % RING], c_ps[:], ACT.Copy).then_inc(c_copied, 1)
                            elif n + B_AHEAD < STEPS:
                                copy_b(w - 1, n + B_AHEAD)
                            elif front:
                                copy_b(w, n + B_AHEAD - STEPS)
                        side_work(w, par, front, scan, back, n, half)
                if front and not scan:
                    for n in range(B_AHEAD):
                        copy_b(w, n)

            bodies(act, body)

        @block.vector
        def _(dve):
            nc.vector.memset(xp_rows, 0.0).then_inc(weights_cleared, 1)
            nc.vector.memset(eps_col[:], EPS)
            nc.vector.memset(eps_sq_col[:], EPS * EPS)
            nc.vector.memset(one_col[:], 1.0)
            nc.vector.memset(fT[:, :, 0:1], 0.0).then_inc(consts_made, 1)
            dve.wait_ge(ident_made, 2)
            nc.vector.tensor_copy(ident_bf[:], ident[:]).then_inc(spread_made, 1)
            dve.wait_ge(spread_made, 1)
            nc.vector.tensor_tensor(pick[:], ident_bf[:, 32:64], ident_bf[:, 64:96], ALU.add).then_inc(spread_made, 1)
            dve.wait_ge(spread_made, 2)
            nc.vector.tensor_tensor(pick[:], pick[:], ident_bf[:, 96:128], ALU.add).then_inc(spread_made, 1)
            dve.wait_ge(spread_made, 3)
            nc.vector.tensor_copy(spread[:], pick[:].unsqueeze(2).to_broadcast([P, 2 * S, P])).then_inc(spread_made, 1)
            def statistics(src, st, semaphore, base, step):
                bn = st["bn"]
                if step < 2:
                    for j in range(step * TILES, (step + 1) * TILES):
                        last = nc.vector.bn_stats(bn[:, j, :], src[:, j, :])
                    if step == 1:
                        last.then_inc(semaphore, 1)
                    return
                dve.wait_ge(semaphore, base + step - 1)
                if step == 2:
                    nc.vector.tensor_tensor(st["dif"][:], bn[:, :, 1], bn[:, :, 4], ALU.subtract)
                    nc.vector.tensor_tensor(st["sum2"][:], bn[:, :, 1], bn[:, :, 4], ALU.add)
                    nc.vector.tensor_tensor(st["m2"][:], bn[:, :, 2], bn[:, :, 5], ALU.add).then_inc(semaphore, 1)
                elif step == 3:
                    nc.vector.tensor_tensor(st["sq"][:], st["dif"][:], st["dif"][:], ALU.mult).then_inc(semaphore, 1)
                else:
                    nc.vector.scalar_tensor_tensor(out=st["var"][:], in0=st["sq"][:], scalar=P / 4.0, in1=st["m2"][:],
                                                   op0=ALU.mult, op1=ALU.add).then_inc(semaphore, 1)

            def front_statistics(e, step):
                if step == 0:
                    dve.wait_ge(xf_in, 16 * (e + 1))
                statistics(xf, st_front, front_stat, 4 * e, step)

            for step in range(5):
                front_statistics(0, step)
            dve.wait_ge(weights_in, 19 * 16)
            for half in range(HALVES):
                for k in range(TAPS):
                    nc.vector.tensor_scalar(tap_w[:, half, k], in_w[:, half, :], conv_taps[:, half, k:k + 1],
                                            None, ALU.mult).then_inc(scaled_w, 1)
            nc.vector.tensor_scalar(one_minus_mu[:], mix_mu[:], -1.0, 1.0, ALU.mult, ALU.add).then_inc(scaled_w, 1)
            dve.wait_ge(a_made, 1)
            nc.vector.tensor_scalar(neg_a[:], neg_a[:], -1.0, None, ALU.mult).then_inc(a_made, 1)
            dve.wait_ge(w_transposed, 1)
            nc.vector.tensor_copy(tap_wT[:, 0], bank[0][:].rearrange("p (k d) -> p k d", d=P))
            nc.vector.tensor_copy(tap_wT[:, 1], bank[1][:].rearrange("p (k d) -> p k d", d=P))
            nc.vector.tensor_copy(z_wT[:], bank[2][:, 0:2 * P].rearrange("p (k d) -> p k d", d=P))
            nc.vector.tensor_copy(xp_wT[:], bank[2][:, 2 * P:].rearrange("p (k d) -> p k d", d=P))
            nc.vector.tensor_copy(out_wT[:], bank[3][:, 0:2 * P].rearrange("p (k d) -> p k d", d=P))
            nc.vector.tensor_copy(dt_wT[:], bank[3][0:RANK, 2 * P:].rearrange("p (k d) -> p k d", d=P))
            nc.vector.tensor_copy(mix_wT[:], bank[4][:, 0:3 * P].rearrange("p (k d) -> p k d", d=P)).then_inc(w_drained, 1)
            dve.wait_ge(w_drained, 1)
            for i in range(2):
                nc.vector.tensor_scalar(mix_now[:, i], mix_wT[:, i], mix_mu[:, i:i + 1], None, ALU.mult)
                nc.vector.tensor_scalar(mix_before[:, i], mix_wT[:, i], one_minus_mu[:, i:i + 1], None,
                                        ALU.mult).then_inc(mix_made, 1)

            nc.vector.tensor_scalar(mix_wT[:, 2], mix_wT[:, 2], 0.5, None, ALU.mult).then_inc(mix_made, 1)

            def shift_of(st, scale, semaphore):
                nc.vector.scalar_tensor_tensor(out=st["shift"][:], in0=st["sum2"][:], scalar=-0.5, in1=scale,
                                               op0=ALU.mult, op1=ALU.mult).then_inc(semaphore, 1)

            def normalize(dst, src, scale, st, bi, semaphore):
                for j in range(bi * TILES, (bi + 1) * TILES):
                    last = nc.vector.tensor_scalar(dst[:, j, :], src[:, j, :], scale[:, j:j + 1],
                                                   st["shift"][:, j:j + 1], ALU.mult, ALU.add)
                last.then_inc(semaphore, 1)

            def make_dbu(pair, par, n):
                if by_pool(n):
                    return
                t = pair * STEPS + n
                bi = n // S
                dve.wait_ge(b_spread, t + 1)
                if n % S == 0:
                    dve.wait_ge((dt_dve, dt_pool)[bi], 2 * pair + 2)
                wait(dve, scanned, 2 * (t + 1 - RING))
                nc.vector.tensor_tensor(dbu[:, n % RING], dtu[par][:, :, bi, :],
                                        b_ps[:].unsqueeze(1).to_broadcast([P, HALVES, L]),
                                        ALU.mult).then_inc(dbu_dve, 1)

            def take_y(e, bi, parity, previous, half):
                if half == 0:
                    dve.wait_ge(y_added, e * STEPS + (bi + 1) * S)
                    wait(dve, filled[bank_of(previous[0])], count_of(*previous))
                last = nc.vector.scalar_tensor_tensor(
                    out=yg[:, half], in0=xc[parity][:, half, bi, :], scalar=d_skip[:, half:half + 1],
                    in1=y_acc[half][:], op0=ALU.mult, op1=ALU.add)
                if half == HALVES - 1:
                    last.then_inc(y_taken, 1)

            def gate_y(e, bi, parity):
                dve.wait_ge(y_taken, 2 * e + bi + 1)
                nc.vector.tensor_tensor(yg[:], yg[:], zs[parity][:, :, bi, :], ALU.mult).then_inc(y_gated, 1)

            def take_v(group, w, bi):
                b = bank_of(group)
                dve.wait_ge(filled[b], count_of(group, w))
                dve.wait_ge(filled[bank_of("back_tr1")], count_of("back_tr1", w - 1 if bi else w))
                for j in range(TILES):
                    jj = bi * TILES + j
                    last = nc.vector.scalar_tensor_tensor(
                        out=v[:, jj, :], in0=xb[:, jj, :], scalar=r1_back[:, jj:jj + 1],
                        in1=misc[b][:, j * P:(j + 1) * P], op0=ALU.mult, op1=ALU.add)
                last.then_inc(drained[b], 1)

            def softplus(e, bi, step):
                base = 6 * e + 3 * bi
                if step == 0:
                    dve.wait_ge(ln_made, 2 * e + bi + 1)
                    wait(dve, soft_made, base)
                    nc.vector.tensor_scalar(soft_lin, soft[:, bi], 1.0, -1.0, ALU.add, ALU.add).then_inc(soft_made, 1)
                elif step == 1:
                    dve.wait_ge(soft_made, base + 1)
                    nc.vector.tensor_tensor(soft_ln[:], soft_ln[:], soft_lin, ALU.subtract).then_inc(soft_made, 1)
                else:
                    dve.wait_ge(soft_made, base + 2)
                    nc.vector.scalar_tensor_tensor(out=soft[:, bi], in0=soft_ln[:], scalar=0.0,
                                                   in1=soft[:, bi], op0=ALU.min, op1=ALU.add).then_inc(soft_made, 1)

            def side_work(w, par, front, scan, back, n, slot):
                q = 3 * n + slot
                if 84 <= q < 89 and front:
                    front_statistics(w + 1, q - 84)
                if q == 0 and front:
                    dve.wait_ge(front_rstd, 2 * w + 2)
                    shift_of(st_front, front_rstds[par][:, 1], front_shift)
                if q in (1, 2) and front:
                    dve.wait_ge(front_shift, w + 1)
                    normalize(hn, xf, front_rstds[par][:, 1], st_front, q - 1, hn_made)
                if n in (23, 24) and front:
                    bi = n - 23
                    b = bank_of(f"xproj{bi}")
                    pt = parts[par][:, bi, :]
                    if slot == 0:
                        dve.wait_ge(hi_made, 2 * w + bi + 1)
                        wait(dve, parts_made, 4 * w + 2 * bi)
                        nc.vector.tensor_tensor(rest[64:P], misc[b][64:P, :], pt[64:P], ALU.subtract).then_inc(drained[b], 1)
                    elif slot == 1:
                        dve.wait_ge(drained[b], count_of(f"xproj{bi}", w))
                        nc.vector.tensor_copy(pt[64:P], rest[64:P]).then_inc(parts_made, 1)
                    else:
                        dve.wait_ge(parts_made, 4 * w + 2 * bi + 1)
                        nc.vector.tensor_tensor(pt[96:P], rest[96:P], pt[96:P], ALU.subtract).then_inc(parts_made, 1)
                if n == 26 and front:
                    softplus(w, 0, slot)
                if q in (26, 27, 29) and scan:
                    softplus(w - 1, 1, (26, 27, 29).index(q))
                if n == 27 and front:
                    if slot == 0:
                        dve.wait_ge(soft_made, 6 * w + 3)
                        nc.vector.tensor_tensor(dt[par][:, :, 0, :], dt[par][:, :, 0, :], soft[:, 0],
                                                ALU.add).then_inc(dt_dve, 1)
                    elif slot == 1:
                        dve.wait_ge(dt_dve, 2 * w + 1)
                        dve.wait_ge(silu_made, 2 * w + 1)
                        nc.vector.tensor_tensor(dtu[par][:, :, 0, :], dt[par][:, :, 0, :],
                                                xc[par][:, :, 0, :], ALU.mult).then_inc(dt_dve, 1)
                if q in (9, 10) and back:
                    take_y(w - 2, 1, par, ("outproj0", w - 1), q - 9)
                if q == 12 and back:
                    gate_y(w - 2, 1, par)
                if q == 19 and back:
                    take_v("outproj1", w, 1)
                if 21 <= q < 25 and back:
                    if q == 21:
                        dve.wait_ge(drained[bank_of("outproj1")], count_of("outproj1", w))
                    statistics(v, st_attn, attn_stat, 4 * (w - 2), q - 20)
                if q == 34 and back:
                    dve.wait_ge(x1_scaled, 2 * (w - 1))
                    dve.wait_ge(xb_in, 16 * (w - 1))
                    nc.vector.tensor_tensor(x1[:], x1[:], xb[:], ALU.add).then_inc(x1_made, 1)
                if q == 30 and back:
                    dve.wait_ge(attn_rstd, 2 * (w - 1))
                    shift_of(st_attn, st_attn["rstd"][:], attn_shift)
                if q in (31, 32) and back:
                    dve.wait_ge(attn_shift, w - 1)
                    dve.wait_ge(out_made, w - 1)
                    normalize(x1, v, st_attn["rstd"], st_attn, q - 31, x1_scaled)
                if 36 <= q < 41 and back:
                    if q == 36:
                        dve.wait_ge(x1_made, w - 1)
                    statistics(x1, st_mid, mid_stat, 4 * (w - 2), q - 36)
                if q == 44 and back:
                    dve.wait_ge(mid_rstd, 2 * (w - 1))
                    shift_of(st_mid, st_mid["rstd"][:], mid_shift)
                if q in (45, 46) and back:
                    dve.wait_ge(mid_shift, w - 1)
                    normalize(f, x1, st_mid["rstd"], st_mid, q - 45, f_made)
                if q in (80, 83) and back:
                    bi = (q - 80) // 3
                    b = bank_of(f"value{bi}")
                    tiles = slice(bi * TILES, (bi + 1) * TILES)
                    dve.wait_ge(filled[b], count_of(f"value{bi}", w))
                    nc.vector.scalar_tensor_tensor(out=o[:, tiles, :], in0=gate[:, tiles, :], scalar=1.0,
                                                   in1=misc[b][:].rearrange("p (j d) -> p j d", d=P),
                                                   op0=ALU.add, op1=ALU.mult).then_inc(drained[b], 1)
                if 86 <= q < 91 and back:
                    if q < 88:
                        g = f"value{q - 86}"
                        dve.wait_ge(drained[bank_of(g)], count_of(g, w))
                    statistics(o, st_out, out_stat, 4 * (w - 2), q - 86)
                if q == 93 and back:
                    dve.wait_ge(out_rstd, 2 * (w - 1))
                    shift_of(st_out, st_out["rstd"][:], out_shift)
                if q in (94, 95) and back:
                    dve.wait_ge(out_shift, w - 1)
                    normalize(o, o, st_out["rstd"], st_out, q - 94, o_scaled)
                if q in (57, 58) and scan:
                    take_y(w - 1, 0, 1 - par, ("outproj1", w), q - 57)
                if q == 59 and scan:
                    gate_y(w - 1, 0, 1 - par)
                if q == 56 and scan:
                    nc.vector.tensor_copy(r1_back[:], front_rstds[1 - par][:, 0]).then_inc(r1_kept, 1)
                if q == 63 and scan:
                    dve.wait_ge(r1_kept, w)
                    dve.wait_ge(xb_in, 16 * w)
                    take_v("outproj0", w, 0)
                    dve.wait_ge(drained[bank_of("outproj0")], count_of("outproj0", w))
                    statistics(v, st_attn, attn_stat, 4 * (w - 1), 0)

            def body(w, par, front, scan, back):
                for n in range(STEPS):
                    if scan and n + DBU_AHEAD < STEPS:
                        make_dbu(w - 1, 1 - par, n + DBU_AHEAD)
                    elif scan and front:
                        make_dbu(w, par, n + DBU_AHEAD - STEPS)
                    side_work(w, par, front, scan, back, n, 0)
                    for half in range(HALVES):
                        if scan:
                            t = (w - 1) * STEPS + n
                            if half == 0:
                                wait(dve, prod_made, t + 1 - RING)
                                if by_pool(n):
                                    dve.wait_ge(dbu_pool, pool_made(w - 1, n) + 1)
                                else:
                                    dve.wait_ge(dbu_dve, dve_made(w - 1, n) + 1)
                            dve.wait_ge(da_made, 2 * t + half + 1)
                            nc.vector.tensor_tensor_scan(h[:, n % RING, half], da[half][:], dbu[:, n % RING, half], 0.0,
                                                         ALU.mult, ALU.add).then_inc(scanned, 1)
                        side_work(w, par, front, scan, back, n, half + 1)
                if front and not scan:
                    for n in range(DBU_AHEAD):
                        make_dbu(w, par, n)

            bodies(dve, body)

        @block.tensor
        def _(pe):
            pe.wait_ge(ident_made, 2)
            pe.wait_ge(weights_in, 19 * 16)
            pe.wait_ge(scaled_w, HALVES * TAPS + 1)
            tr = lambda dst, src: nc.tensor.transpose(dst, src, ident[:])
            for half in range(HALVES):
                cols = slice(half * P, (half + 1) * P)
                for k in range(TAPS):
                    tr(bank[half][:, k * P:(k + 1) * P], tap_w[:, half, k])
                tr(bank[2][:, cols], in_w[:, 2 + half, :])
                tr(bank[2][:, 2 * P + half * P:2 * P + (half + 1) * P], xp_rows[:, cols])
                tr(bank[3][:, cols], out_w[:, cols])
                tr(bank[3][0:RANK, 2 * P + half * P:2 * P + (half + 1) * P], dt_w_rows[:, half, :])
            for i in range(3):
                last = tr(bank[4][:, i * P:(i + 1) * P], mix_w[:, i, :])
            last.then_inc(w_transposed, 1)
            pe.wait_ge(w_drained, 1)
            pe.wait_ge(mix_made, 3)
            pe.wait_ge(spread_made, 4)
            pe.wait_ge(consts_made, 1)

            def bank_free(group, w):
                b = bank_of(group)
                wait(pe, drained[b], count_of(group, w) - 1)
                return misc[b]

            def done(group, last):
                last.then_inc(filled[bank_of(group)], 1)

            def skip(groups, w):
                for g in groups:
                    bank_free(g, w)
                    pe.sem_inc(filled[bank_of(g)], 1)
                    pe.sem_inc(drained[bank_of(g)], 1)

            def evacuated(group, w):
                pe.wait_ge(drained[bank_of(group)], count_of(group, w))

            def spread_b(pair, par, n):
                bi, s = n // S, n % S
                if s == 0:
                    pe.wait_ge(parts_made, 4 * pair + 2 * bi + 2)
                before = pair * STEPS + n - 1
                if not isinstance(before, int) or before >= 0:
                    if by_pool(n - 1):
                        pe.wait_ge(b_copied, pool_made(pair, n))
                    else:
                        pe.wait_ge(dbu_dve, dve_made(pair, n))
                nc.tensor.matmul(b_ps[:], spread[:, s, :], parts[par][:, bi, :],
                                 start=True, stop=True).then_inc(b_spread, 1)

            def spread_c(pair, par, n):
                bi, s = n // S, n % S
                wait(pe, c_copied, pair * STEPS + n)
                nc.tensor.matmul(c_ps[:], spread[:, S + s, :], parts[par][:, bi, :],
                                 start=True, stop=True).then_inc(c_spread, 1)

            def add_states(w, n):
                t = (w - 1) * STEPS + n
                s = n % S
                if s == 0:
                    wait(pe, y_taken, 2 * (w - 1) + n // S)
                pe.wait_ge(prod_made, t + 1)
                for half in range(HALVES):
                    last = nc.tensor.matmul(y_acc[half][:], ident[:], prod[:, n % RING, half],
                                            start=(s == 0), stop=(s == S - 1))
                last.then_inc(y_added, 1)

            def transposes(group, w, src, bi):
                dst = bank_free(group, w)
                for j in range(TILES):
                    last = nc.tensor.transpose(dst[:, j * P:(j + 1) * P], src[:, bi * TILES + j, :], ident[:])
                done(group, last)

            def out_project(group, w, part):
                dst = bank_free(group, w) if part == 0 else misc[bank_of(group)]
                for j in range(2 * part, 2 * part + 2):
                    for half in range(HALVES):
                        last = nc.tensor.matmul(dst[:, j * P:(j + 1) * P], yg[:, half, j * P:(j + 1) * P],
                                                out_wT[:, half, :], start=(half == 0), stop=(half == HALVES - 1))
                if part == 1:
                    done(group, last)

            def mix_key(bi, w):
                g = f"key{bi}"
                evacuated(f"back_tr{bi}", w)
                dst = bank_free(g, w)
                nc.tensor.matmul(dst[:], mix_now[:, 1], fT[:, bi, 1:L + 1], start=True, stop=False)
                done(g, nc.tensor.matmul(dst[:], mix_before[:, 1], fT[:, bi, 0:L], start=False, stop=True))

            def mix_gate(bi, w):
                g = f"gate{bi}"
                dst = bank_free(g, w)
                for j in range(TILES):
                    nc.tensor.matmul(dst[:, j * P:(j + 1) * P], fT[:, bi, j * P + 1:(j + 1) * P + 1],
                                     mix_now[:, 0], start=True, stop=False)
                    last = nc.tensor.matmul(dst[:, j * P:(j + 1) * P], fT[:, bi, j * P:(j + 1) * P],
                                            mix_before[:, 0], start=False, stop=True)
                done(g, last)

            def side_work(w, par, front, scan, back, n, slot):
                if n == 5:
                    if back:
                        pe.wait_ge(y_gated, 2 * (w - 1))
                        out_project("outproj1", w, slot)
                    elif slot == 0:
                        skip(["outproj1"], w)
                if n == 1:
                    if front:
                        pe.wait_ge(hn_made, 2 * w + slot + 1)
                        transposes(f"front_tr{slot}", w, hn, slot)
                    else:
                        skip([f"front_tr{slot}"], w)
                if 3 <= n < 12 and n != 5 and front:
                    k = 2 * (n - 3 - (n > 5)) + slot
                    bi, half, back_by = k // (2 * TAPS), k // TAPS % 2, k % TAPS
                    g = f"conv{bi}{half}"
                    if back_by == 0:
                        evacuated(f"front_tr{bi}", w)
                        bank_free(g, w)
                    last = nc.tensor.matmul(misc[bank_of(g)][:, back_by:L], tap_wT[:, half, TAPS - 1 - back_by],
                                            hT[:, bi, 0:L - back_by], start=(back_by == 0),
                                            stop=(back_by == TAPS - 1))
                    if back_by == TAPS - 1:
                        done(g, last)
                if 12 <= n < 16 and slot == 0 and front:
                    bi, half = (n - 12) // 2, (n - 12) % 2
                    g = f"z{bi}{half}"
                    done(g, nc.tensor.matmul(bank_free(g, w)[:], z_wT[:, half], hT[:, bi, :], start=True, stop=True))
                if (n, slot) == (4, 1) and not front:
                    skip(["conv00"], w)
                if (n, slot) == (15, 0) and not front:
                    skip([f"{a}{bi}{half}" for a in ("conv", "z") for bi in range(2) for half in range(2)][1:], w)
                if (n, slot) in ((15, 1), (16, 0)):
                    bi = 1 - slot
                    if back:
                        pe.wait_ge(f_made, 2 * (w - 2) + bi + 1)
                        transposes(f"back_tr{bi}", w, f, bi)
                    else:
                        skip([f"back_tr{bi}"], w)
                if back:
                    if (n, slot) == (17, 0):
                        mix_key(0, w)
                    if (n, slot) == (17, 1):
                        mix_key(1, w)
                    if (n, slot) == (18, 1):
                        mix_gate(0, w)
                    if (n, slot) == (19, 0):
                        mix_gate(1, w)
                elif (n, slot) == (19, 0):
                    skip(["key0", "key1", "gate0", "gate1"], w)
                if (n, slot) == (20, 0):
                    if scan:
                        pe.wait_ge(y_gated, 2 * (w - 1) + 1)
                        out_project("outproj0", w, 0)
                        out_project("outproj0", w, 1)
                    else:
                        skip(["outproj0"], w)
                if (n, slot) in ((20, 1), (21, 0), (21, 1), (22, 0)):
                    bi, half = n - 20 - (slot == 0), 1 - slot
                    g = f"xproj{bi}"
                    if front:
                        if half == 0:
                            pe.wait_ge(silu_made, 2 * w + 1)
                            bank_free(g, w)
                        last = nc.tensor.matmul(misc[bank_of(g)][:], xp_wT[:, half], xc[par][:, half, bi, :],
                                                start=(half == 0), stop=(half == HALVES - 1))
                        if half == 1:
                            done(g, last)
                    elif half == 0:
                        skip([g], w)
                if n in (23, 27):
                    bi, half = (n - 23) // 4, slot
                    g = f"dt{bi}{half}"
                    if front:
                        pe.wait_ge(hi_made, 2 * w + bi + 1)
                        done(g, nc.tensor.matmul(bank_free(g, w)[:], dt_wT[:, half], dt_low[:, bi, :],
                                                 start=True, stop=True))
                    else:
                        skip([g], w)
                if n == 25:
                    g = f"value{slot}"
                    if back:
                        pe.wait_ge(key_squared, w - 1)
                        dst = bank_free(g, w)
                        for j in range(TILES):
                            last = nc.tensor.matmul(dst[:, j * P:(j + 1) * P], key[:, slot, j * P:(j + 1) * P],
                                                    mix_wT[:, 2], start=True, stop=True)
                        done(g, last)
                    else:
                        skip([g], w)

            def body(w, par, front, scan, back):
                for n in range(STEPS):
                    if scan:
                        if n + B_AHEAD < STEPS:
                            spread_b(w - 1, 1 - par, n + B_AHEAD)
                        elif front:
                            spread_b(w, par, n + B_AHEAD - STEPS)
                    side_work(w, par, front, scan, back, n, 0)
                    if scan:
                        if n + 1 < STEPS:
                            spread_c(w - 1, 1 - par, n + 1)
                        elif front:
                            spread_c(w, par, 0)
                    if scan and n >= LAG:
                        add_states(w, n - LAG)
                    if n < LAG and back:
                        add_states(w - 1, n - LAG + STEPS)
                    side_work(w, par, front, scan, back, n, 1)
                if front and not scan:
                    spread_c(w, par, 0)
                    for n in range(B_AHEAD):
                        spread_b(w, par, n)

            bodies(pe, body)


_INS = ["L0_attn_x", "L0_attn_ln_gamma", "L0_attn_ln_beta", "L0_attn_in_proj_w", "L0_attn_conv_w",
        "L0_attn_conv_b", "L0_attn_x_proj_w", "L0_attn_dt_proj_w", "L0_attn_dt_proj_b", "L0_attn_A_log",
        "L0_attn_D", "L0_attn_out_proj_w", "L0_ffn_W_r", "L0_ffn_W_k", "L0_ffn_W_v", "L0_ffn_mu_r",
        "L0_ffn_mu_k"]


def kernel(**inputs):
    import numpy as np
    import concourse.bacc as bacc
    from concourse import mybir as _mybir
    from concourse.bass_utils import run_bass_kernel_spmd

    nc = bacc.Bacc("TRN2", target_bir_lowering=False, num_devices=1)
    arrays, args = {}, []
    for name in _INS:
        a = np.ascontiguousarray(inputs[name])
        arrays[f"in_{name}"] = a
        args.append(nc.dram_tensor(f"in_{name}", a.shape, _mybir.dt.from_np(a.dtype), kind="ExternalInput").ap())
    shape = inputs["L0_attn_x"].shape
    args.append(nc.dram_tensor("out", shape, _mybir.dt.float32, kind="ExternalOutput").ap())
    mamba_sandwich(nc, *args)
    r = run_bass_kernel_spmd(nc, [arrays], core_ids=[0])
    return r.results[0]["out"]
```
